# Optimizing a Trainium2 kernel written in Bass

```python
import numpy as np
import jax
import jax.numpy as jnp

def _softmax(x, axis=-1):
    return jax.nn.softmax(x, axis=axis)

def _gelu(x):
    return jax.nn.gelu(x, approximate=True)

def _silu(x):
    return jax.nn.silu(x)

def _sigmoid(x):
    return jax.nn.sigmoid(x)

def _layernorm(x, axis=-1, eps=1e-05):
    m = jnp.mean(x, axis=axis, keepdims=True)
    v = jnp.var(x, axis=axis, keepdims=True)
    return (x - m) / jnp.sqrt(v + eps)

def _scatter_add(tgt, idx, src, axis=0):
    return tgt.at[idx].add(src)

def _segment_sum(src, seg, n):
    return jax.ops.segment_sum(src, seg, n)
kernel_name = 'mk_macaron_d1_jaxref_r8_585781'

def setup_inputs(seed: int=0):
    np.random.seed(seed)
    _w = jnp.asarray

    def _L0_attn_setup():
        import jax, jax.numpy as jnp
        import numpy as np
        B, T, C = (2, 256, 256)
        NH, NKV = (16, 4)
        HD = C // NH

        def _rope(x):
            D = x.shape[-1]
            t = x.shape[-2]
            inv_freq = 1.0 / 10000.0 ** (jnp.arange(0, D, 2, dtype=jnp.float32) / D)
            freqs = jnp.arange(t, dtype=jnp.float32)[:, None] * inv_freq[None, :]
            emb = jnp.concatenate([freqs, freqs], axis=-1)
            cos, sin = (jnp.cos(emb), jnp.sin(emb))
            x1, x2 = (x[..., :D // 2], x[..., D // 2:])
            rotated = jnp.concatenate([-x2, x1], axis=-1)
            return x * cos + rotated * sin
        key = jax.random.key(seed)
        ks = jax.random.split(key, 5)
        w = lambda k, shape: jax.random.normal(k, shape, jnp.float32) * 0.02
        return {'x': jax.random.normal(ks[0], (B, T, C), jnp.float32), 'Wq': w(ks[1], (C, C)), 'Wk': w(ks[2], (C, NKV * HD)), 'Wv': w(ks[3], (C, NKV * HD)), 'Wproj': w(ks[4], (C, C))}
    _L0_attn_in = _L0_attn_setup()

    def _L0_ffn_setup():
        import jax, jax.numpy as jnp
        import numpy as np
        DIM = 256
        HID = 704
        ZERO_POINT = 128.0

        def _qlinear(x, wq, scale):
            W = (wq.astype(jnp.float32) - ZERO_POINT) * scale[:, None]
            return jnp.einsum('bsd,hd->bsh', x, W)
        key = jax.random.key(seed)
        ks = jax.random.split(key, 7)
        B, S = (4, 256)
        sg = jax.random.uniform(ks[1], (HID,)) * (0.02 / np.sqrt(DIM)) + 0.0001
        su = jax.random.uniform(ks[3], (HID,)) * (0.02 / np.sqrt(DIM)) + 0.0001
        sd = jax.random.uniform(ks[5], (DIM,)) * (0.02 / np.sqrt(HID)) + 0.0001
        return {'x': jax.random.normal(ks[0], (B, S, DIM), dtype=jnp.float32), 'wq_gate': jax.random.randint(ks[2], (HID, DIM), 0, 32, dtype=jnp.int32), 's_gate': sg, 'wq_up': jax.random.randint(ks[4], (HID, DIM), 0, 32, dtype=jnp.int32), 's_up': su, 'wq_down': jax.random.randint(ks[6], (DIM, HID), 0, 32, dtype=jnp.int32), 's_down': sd}
    _L0_ffn_in = _L0_ffn_setup()
    _d = {'L0_attn_x': _L0_attn_in['x'], 'L0_attn_Wq': _L0_attn_in['Wq'], 'L0_attn_Wk': _L0_attn_in['Wk'], 'L0_attn_Wv': _L0_attn_in['Wv'], 'L0_attn_Wproj': _L0_attn_in['Wproj'], 'L0_ffn_wq_gate': _L0_ffn_in['wq_gate'], 'L0_ffn_s_gate': _L0_ffn_in['s_gate'], 'L0_ffn_wq_up': _L0_ffn_in['wq_up'], 'L0_ffn_s_up': _L0_ffn_in['s_up'], 'L0_ffn_wq_down': _L0_ffn_in['wq_down'], 'L0_ffn_s_down': _L0_ffn_in['s_down']}
    _x0 = _d['L0_attn_x']
    _d['L0_attn_x'] = jax.random.normal(jax.random.fold_in(jax.random.key(seed), 1), (4, 512, 256), dtype=_x0.dtype)
    del _x0
    return _d

def reference(L0_attn_x, L0_attn_Wq, L0_attn_Wk, L0_attn_Wv, L0_attn_Wproj, L0_ffn_wq_gate, L0_ffn_s_gate, L0_ffn_wq_up, L0_ffn_s_up, L0_ffn_wq_down, L0_ffn_s_down):

    def _L0_attn_ref(x, Wq, Wk, Wv, Wproj):
        import jax, jax.numpy as jnp
        import numpy as np
        B, T, C = (2, 256, 256)
        NH, NKV = (16, 4)
        HD = C // NH

        def _rope(x):
            D = x.shape[-1]
            t = x.shape[-2]
            inv_freq = 1.0 / 10000.0 ** (jnp.arange(0, D, 2, dtype=jnp.float32) / D)
            freqs = jnp.arange(t, dtype=jnp.float32)[:, None] * inv_freq[None, :]
            emb = jnp.concatenate([freqs, freqs], axis=-1)
            cos, sin = (jnp.cos(emb), jnp.sin(emb))
            x1, x2 = (x[..., :D // 2], x[..., D // 2:])
            rotated = jnp.concatenate([-x2, x1], axis=-1)
            return x * cos + rotated * sin
        b, t, c = x.shape
        q = (x @ Wq).reshape(b, t, NH, HD).transpose(0, 2, 1, 3)
        k = (x @ Wk).reshape(b, t, NKV, HD).transpose(0, 2, 1, 3)
        v = (x @ Wv).reshape(b, t, NKV, HD).transpose(0, 2, 1, 3)
        q = _rope(q)
        k = _rope(k)
        rep = NH // NKV
        k = jnp.repeat(k, rep, axis=1)
        v = jnp.repeat(v, rep, axis=1)
        scale = 1.0 / jnp.sqrt(jnp.float32(HD))
        scores = jnp.einsum('bhqd,bhkd->bhqk', q, k) * scale
        causal = jnp.tril(jnp.ones((t, t), dtype=bool))
        scores = jnp.where(causal, scores, jnp.finfo(scores.dtype).min)
        attn = jax.nn.softmax(scores, axis=-1)
        y = jnp.einsum('bhqk,bhkd->bhqd', attn, v)
        y = y.transpose(0, 2, 1, 3).reshape(b, t, c)
        return y @ Wproj

    def _L0_ffn_ref(x, wq_gate, s_gate, wq_up, s_up, wq_down, s_down):
        import jax, jax.numpy as jnp
        import numpy as np
        DIM = 256
        HID = 704
        ZERO_POINT = 128.0

        def _qlinear(x, wq, scale):
            W = (wq.astype(jnp.float32) - ZERO_POINT) * scale[:, None]
            return jnp.einsum('bsd,hd->bsh', x, W)
        gate = _qlinear(x, wq_gate, s_gate)
        gate = jax.nn.silu(gate)
        up = _qlinear(x, wq_up, s_up)
        return _qlinear(gate * up, wq_down, s_down)
    x = L0_attn_x
    x = x + 0.5 * _L0_ffn_ref(_layernorm(x, axis=-1), L0_ffn_wq_gate, L0_ffn_s_gate, L0_ffn_wq_up, L0_ffn_s_up, L0_ffn_wq_down, L0_ffn_s_down)
    x = x + _L0_attn_ref(_layernorm(x, axis=-1), L0_attn_Wq, L0_attn_Wk, L0_attn_Wv, L0_attn_Wproj)
    x = x + 0.5 * _L0_ffn_ref(_layernorm(x, axis=-1), L0_ffn_wq_gate, L0_ffn_s_gate, L0_ffn_wq_up, L0_ffn_s_up, L0_ffn_wq_down, L0_ffn_s_down)
    return x

_drawn_inputs = setup_inputs


def setup_inputs(seed=0):
    import zlib

    import numpy as np

    out = dict(_drawn_inputs(seed))
    spreads = {}
    factors = {'L0_attn_Wq': 8.0,
     'L0_attn_Wk': 8.0,
     'L0_attn_Wv': 4.586,
     'L0_attn_Wproj': 4.811,
     'L0_ffn_s_gate': 8.0,
     'L0_ffn_s_up': 8.0,
     'L0_ffn_s_down': 8.0}
    for name, (base, spread) in spreads.items():
        noise = np.random.default_rng([zlib.crc32(name.encode()), seed]).standard_normal(out[name].shape)
        drawn = base * np.exp(spread * noise) if base else spread * noise
        out[name] = jnp.asarray(drawn.astype(out[name].dtype))
    for name, factor in factors.items():
        out[name] = (out[name] * factor).astype(out[name].dtype)
    return out
```

```python
from contextlib import ExitStack

import concourse.bass as bass
from concourse import mybir

F32 = mybir.dt.float32
F32R = mybir.dt.float32r
BF16 = mybir.dt.bfloat16
I32 = mybir.dt.int32
ACT = mybir.ActivationFunctionType
ALU = mybir.AluOpType
AX = mybir.AxisListType

P = 128
B, T, C = 4, 512, 256
HEADS, KV, HD = 16, 4, 16
HID = 704
NT = T // P
KC = C // P
FULL = HID // P
REST = HID - FULL * P
HT = FULL + 1
QKV = C + 2 * KV * HD
QK = C + KV * HD
ROT = HEADS + KV
ST = 64
UNITS_S = 12
UNITS_P = 10
VW = 32
PASSES = 3
NEG = -3.0e38
EPS = 1e-5


def score_units():
    units = [(0, (0, 2)), (0, (1, 3)), (1, (0, 2)), (1, (1, 3))]
    return units + [(j, (h,)) for j in (2, 3) for h in range(4)]


def prob_units():
    return ([[(h, 0, 0)] for h in range(4)] + [[(h, 1, 0), (h, 3, 384)] for h in range(4)]
            + [[(h, 2, 0), (h + 2, 2, 256)] for h in range(2)])


def prob_place(h, kt, j):
    if kt == 0:
        return h, P * j
    if kt == 1:
        return 4 + h, P * (j - 1)
    if kt == 3:
        return 4 + h, 384
    return 8 + h % 2, 256 * (h // 2) + P * (j - 2)


def build(nc, x, wq, wk, wv, wproj, w_gate, s_gate, w_up, s_up, w_down, s_down, rope, out):
    with ExitStack() as ctx:
        def sb(name, shape, dt=F32):
            return ctx.enter_context(nc.sbuf_tensor(name, shape, dt))

        def sem(name):
            return ctx.enter_context(nc.semaphore(name))

        bank = [ctx.enter_context(nc.psum_tensor(f"bank{i}", [P, 512], F32)) for i in range(8)]
        gu_bank = bank[0:4]
        tr_bank = bank[4:6]
        down_bank = bank[6:8]
        s_bank = bank[0:3]
        p_bank = bank[3:6]
        pv_bank, m_bank = bank[6], bank[7]

        X = sb("X", [P, B * NT, C])
        xn = sb("xn", [P, NT, C])
        stats = sb("stats", [P, NT, 6])
        mv = sb("mv", [P, NT, 2])
        part_sum = sb("part_sum", [P, NT, 16])
        row_sum = sb("row_sum", [P, NT])
        mean = sb("mean", [P, NT])
        inv_c = sb("inv_c", [P, NT])
        veps = sb("veps", [P, NT])
        rstd = sb("rstd", [P, NT])
        neg_half = sb("neg_half", [P, NT])
        eps = sb("eps", [P, NT])
        xh = sb("xh", [P, KC, T], F32R)
        xl = sb("xl", [P, KC, T], F32R)
        ident = sb("ident", [P, P])
        ident_b = sb("ident_b", [P, P], BF16)
        causal_b = sb("causal_b", [P, P], BF16)

        pT = sb("pT", [P, 2, UNITS_P, 512])
        raw = pT[:, :, :, :].rearrange("p a u n -> p (a u n)")
        n_gu, n_d = (2 * FULL + 1) * C, KC * HID
        wi = raw[:, 0:n_gu].bitcast(I32).rearrange("p (m c) -> p m c", c=C)
        wf = raw[:, n_gu:2 * n_gu].rearrange("p (m c) -> p m c", c=C)
        wdi = raw[:, 2 * n_gu:2 * n_gu + n_d].bitcast(I32).rearrange("p (m c) -> p m c", c=HID)
        wdf = raw[:, 2 * n_gu + n_d:2 * (n_gu + n_d)].rearrange("p (m c) -> p m c", c=HID)
        n_end = 2 * (n_gu + n_d)
        guh = sb("guh", [P, KC, 2 * HID], F32R)
        gul = sb("gul", [P, KC, 2 * HID], F32R)
        dh = sb("dh", [P, HT, C], F32R)
        dl = sb("dl", [P, HT, C], F32R)
        s_gu = sb("s_gu", [P, 2 * FULL + 1])
        sd_raw = raw[:, n_end + KC * QKV + KC * C:n_end + KC * QKV + KC * C + C]
        sd_half = sb("sd_half", [P, C])
        w3 = raw[:, n_end:n_end + KC * QKV].rearrange("p (k n) -> p k n", n=QKV)
        w3h = sb("w3h", [P, KC, QKV], F32R)
        w3l = sb("w3l", [P, KC, QKV], F32R)
        wp = raw[:, n_end + KC * QKV:n_end + KC * QKV + KC * C].rearrange("p (k n) -> p k n", n=C)
        wph = sb("wph", [P, KC, C], F32R)
        wpl = sb("wpl", [P, KC, C], F32R)
        cs = sb("cs", [P, NT, 2, HD])

        sg = sb("sg", [P, 2, T])
        hf = sb("hf", [P, 2, T])
        hh = sb("hh", [P, HT, T], F32R)
        hl = sb("hl", [P, HT, T], F32R)
        delta = sb("delta", [P, 2, C])

        def idle(buffer):
            return buffer[:, :, 0:ROT * HD].rearrange("p s (h d) -> p s h d", d=HD)
        rot_a, rot_b = idle(sg), idle(hf)
        rot = sb("rot", [P, 2, ROT, HD])
        qtok = sb("qtok", [P, NT, HEADS, ST])
        ktok = sb("ktok", [P, NT, KV, 2, ST])
        vtok = sb("vtok", [P, NT, KV, VW])
        qst = sb("qst", [P, HEADS // 2, T], F32R)
        kst = sb("kst", [P, KV, T], F32R)
        mneg = sb("mneg", [P, 2, NT, 4])
        mpart = sb("mpart", [P, 2, NT, 2, 2, 2])
        mT = hl[0:8, KC:KC + 2, :]
        rec = sb("rec", [P, 16])
        o_sb = hf[:, 0, :]
        ytok = sb("ytok", [P, NT, C])
        yh, yl = hh[:, 0:KC, :], hl[:, 0:KC, :]

        x0_in, x_in, w_in, c_in = sem("x0_in"), sem("x_in"), sem("w_in"), sem("c_in")
        const = sem("const")
        const_b = sem("const_b")
        pads = sem("pads")
        wf_ready = sem("wf_ready")
        wT_ready, wTh_done, wTl_done = sem("wT_ready"), sem("wTh_done"), sem("wTl_done")
        w3h_done, w3l_done = sem("w3h_done"), sem("w3l_done")
        stats_done, mv_done, veps_done, rstd_done = (sem(n) for n in ("stats_done", "mv_done", "veps_done", "rstd_done"))
        xn_done, xT_ready, xh_done, xl_done = (sem(n) for n in ("xn_done", "xT_ready", "xh_done", "xl_done"))
        gate_ready, up_ready, silu_done = sem("gate_ready"), sem("up_ready"), sem("silu_done")
        h_done, hh_done, hl_done, down_done = (sem(n) for n in ("h_done", "hh_done", "hl_done", "down_done"))
        delta_done, x_done = sem("delta_done"), sem("x_done")
        qkv_ready, v_done, rot_ab, rot_done = (sem(n) for n in ("qkv_ready", "v_done", "rot_ab", "rot_done"))
        hi_done, lo_done = sem("hi_done"), sem("lo_done")
        stack_ready, stack_act, stack_dve = sem("stack_ready"), sem("stack_act"), sem("stack_dve")
        s_ready, smax_done = sem("s_ready"), sem("smax_done")
        mh_done, ml_done, mT_ready, mT_done = (sem(n) for n in ("mh_done", "ml_done", "mT_ready", "mT_done"))
        m_rows = [sem("m_rows0"), sem("m_rows1")]
        p_ready, exp_done, sel_done, pv_done = (sem(n) for n in ("p_ready", "exp_done", "sel_done", "pv_done"))
        o_done, oT_ready, rec_done, y_done = (sem(n) for n in ("o_done", "oT_ready", "rec_done", "y_done"))
        yT_ready, yh_done, yl_done, proj_ready = (sem(n) for n in ("yT_ready", "yh_done", "yl_done", "proj_ready"))
        stored = sem("stored")
        sum_done = sem("sum_done")
        dve_turn, pool_turn = sem("dve_turn"), sem("pool_turn")

        x_rows = x.rearrange("b (t p) c -> p (b t) c", p=P)
        out_rows = out.rearrange("b (t p) c -> p (b t) c", p=P)
        W_DMAS = 4 + 2 + 4 + 1
        C_DMAS = 5
        PRIMED = 1
        primed = dict(pe=[down_done, mT_ready, pv_done], dve=[h_done, x_done, yl_done, mT_done, y_done, ml_done],
                      act=[hi_done, o_done], pool=[hl_done, lo_done, rot_done])
        X_PER_CHUNK = 2

        def tiles(c, first, count):
            return bass.ds(c * NT + first, count)

        def loop(eng, body):
            with eng.Fori(0, B - 1) as c:
                body(c, c + 1)
            body(B - 1, 0)

        block = ctx.enter_context(nc.Block())

        @block.sync
        def _(sp):
            sp.dma_start(X[:, 0:NT, :], x_rows[:, 0:NT, :]).then_inc(x0_in, 16)
            sp.dma_start(wi[:, 0:FULL, :], w_gate[0:FULL * P, :].rearrange("(m p) c -> p m c", p=P)).then_inc(w_in, 16)
            sp.dma_start(wi[REST:P, FULL, :], w_gate[FULL * P:HID, :]).then_inc(w_in, 16)
            sp.dma_start(wi[0:REST, FULL, :], w_up[FULL * P:HID, :]).then_inc(w_in, 16)
            sp.dma_start(wi[:, FULL + 1:, :], w_up[0:FULL * P, :].rearrange("(m p) c -> p m c", p=P)).then_inc(w_in, 16)
            sp.dma_start(wdi[:, :, :], w_down.rearrange("(m p) h -> p m h", p=P)).then_inc(w_in, 16)
            sp.dma_start(sd_raw[:, :], s_down.rearrange("(a c) -> a c", a=1).to_broadcast([P, C])).then_inc(w_in, 16)
            with nc.allow_non_contiguous_dma("scales, one per hidden row"):
                sp.dma_start(s_gu[:, 0:FULL], s_gate[0:FULL * P].rearrange("(m p) -> p m", p=P)).then_inc(w_in, 16)
                sp.dma_start(s_gu[REST:P, FULL:FULL + 1], s_gate[FULL * P:HID].rearrange("(p a) -> p a", a=1)).then_inc(w_in, 16)
                sp.dma_start(s_gu[0:REST, FULL:FULL + 1], s_up[FULL * P:HID].rearrange("(p a) -> p a", a=1)).then_inc(w_in, 16)
                sp.dma_start(s_gu[:, FULL + 1:], s_up[0:FULL * P].rearrange("(m p) -> p m", p=P)).then_inc(w_in, 16)
            sp.dma_start(X[:, NT:, :], x_rows[:, NT:, :]).then_inc(x_in, 16)
            sp.dma_start(w3[:, :, 0:C], wq.rearrange("(k p) n -> p k n", p=P)).then_inc(c_in, 16)
            sp.dma_start(w3[:, :, C:QK], wk.rearrange("(k p) n -> p k n", p=P)).then_inc(c_in, 16)
            sp.dma_start(w3[:, :, QK:QKV], wv.rearrange("(k p) n -> p k n", p=P)).then_inc(c_in, 16)
            sp.dma_start(wp[:, :, :], wproj.rearrange("(k p) n -> p k n", p=P)).then_inc(c_in, 16)
            sp.dma_start(cs[:, :, :, :], rope).then_inc(c_in, 16)

            for s in m_rows:
                sp.sem_inc(s, 16 * PRIMED)

            def batch(b):
                for g in range(KV):
                    sp.wait_ge(mT_done, PRIMED + KV * b + g + 1)
                    for half in range(2):
                        for pair in range(2):
                            row = ST * half + 3 * HD
                            src = 4 * half + 2 * pair
                            sp.dma_start(qst[row:row + 2, 2 * g + pair, :].bitcast(F32),
                                         mT[src:src + 2, g % 2, :].bitcast(F32)).then_inc(m_rows[g % 2], 16)

            with sp.Fori(0, B) as b:
                batch(b)

            with sp.Fori(0, B) as c:
                sp.wait_ge(x_done, PRIMED + 2 * B * X_PER_CHUNK + X_PER_CHUNK * (c + 1))
                sp.dma_start(out_rows[:, tiles(c, 0, NT), :], X[:, tiles(c, 0, NT), :]).then_inc(stored, 16)
            sp.wait_ge(stored, 16 * B)

        @block.tensor
        def _(pe):
            def split3(acc, ah, al, bh, bl, start, stop, check=False):
                pe.matmul(acc, ah, bh, start=start, stop=False, skip_group_check=check)
                pe.matmul(acc, ah, bl, start=False, stop=False, skip_group_check=check)
                return pe.matmul(acc, al, bh, start=False, stop=stop, skip_group_check=check)

            def transpose_weights():
                pe.wait_ge(const, 2)
                n = 0
                for k in range(KC):
                    for first in range(0, 2 * FULL + 1, 4):
                        pe.wait_ge(wf_ready, 1)
                        if n >= 4:
                            pe.wait_ge(wTl_done, n - 3)
                        width = min(4, 2 * FULL + 1 - first)
                        for m in range(width):
                            last = pe.transpose(gu_bank[n % 4][:, P * m:P * m + P],
                                                wf[:, first + m, P * k:P * k + P], ident[:, :])
                        last.then_inc(wT_ready, 1)
                        n += 1
                pe.wait_ge(wf_ready, 2)
                for kt in range(0, HT, 2):
                    pe.wait_ge(wTl_done, n - 3)
                    for i in range(2):
                        for m in range(KC):
                            rows = P if kt + i < FULL else REST
                            last = pe.transpose(gu_bank[n % 4][0:rows, C * i + P * m:C * i + P * m + P],
                                                wdf[:, m, P * (kt + i):P * (kt + i) + rows], ident[:, :])
                    last.then_inc(wT_ready, 1)
                    n += 1

            def transpose_x(n):
                pe.wait_ge(xn_done, NT * n + NT)
                pe.wait_ge(xl_done, KC * n)
                for k in range(KC):
                    for t in range(NT):
                        last = pe.transpose(tr_bank[k][:, P * t:P * t + P], xn[:, t, P * k:P * k + P], ident[:, :])
                    last.then_inc(xT_ready, 1)

            def ffn(base, stage):
                def hidden(n, acc, m):
                    for k in range(KC):
                        cols = slice(P * m, P * m + P)
                        last = split3(acc, guh[:, k, cols], gul[:, k, cols], xh[:, k, :], xl[:, k, :],
                                      start=(k == 0), stop=(k == KC - 1))
                    return last

                def gate_up(n, i):
                    pe.wait_ge(h_done, PRIMED + HT * n + max(i - 1, 0))
                    if i < FULL:
                        hidden(n, gu_bank[2 * i % 4][:, :], i).then_inc(gate_ready, 1)
                        hidden(n, gu_bank[(2 * i + 1) % 4][:, :], FULL + 1 + i).then_inc(up_ready, 1)
                    else:
                        hidden(n, gu_bank[2 * i % 4][:, :], FULL).then_inc(gate_ready, 1)

                def down(n, kt):
                    pe.wait_ge(hl_done, PRIMED + HT * n + kt + 1)
                    rows = P if kt < FULL else REST
                    for t in range(NT):
                        cols = slice(P * t, P * t + P)
                        last = split3(down_bank[t // 2][:, C * (t % 2):C * (t % 2) + C],
                                      hh[0:rows, kt, cols], hl[0:rows, kt, cols], dh[0:rows, kt, :], dl[0:rows, kt, :],
                                      start=(kt == 0 and t % 2 == 0), stop=(kt == HT - 1), check=True)
                    last.then_inc(down_done, 1)

                def chunk(c, following):
                    n = c + base
                    pe.wait_ge(xl_done, KC * (c + stage * B) + KC)
                    gate_up(n, 0)
                    gate_up(n, 1)
                    gate_up(n, 2)
                    pe.wait_ge(x_done, PRIMED + X_PER_CHUNK * (c + stage * B))
                    down(n, 0)
                    gate_up(n, 3)
                    down(n, 1)
                    gate_up(n, 4)
                    down(n, 2)
                    gate_up(n, 5)
                    if following is not None:
                        transpose_x(c + stage * B + 1)
                    for kt in range(3, HT):
                        down(n, kt)

                if stage == 0:
                    loop(pe, chunk)
                else:
                    with pe.Fori(0, B - 1) as c:
                        chunk(c, c + 1)
                    chunk(B - 1, None)

            def attention():
                def qkv(b):
                    pe.wait_ge(xl_done, KC * (b + B) + KC)
                    pe.wait_ge(x_done, PRIMED + X_PER_CHUNK * (b + B))
                    pe.wait_ge(yl_done, PRIMED + KC * b)
                    for t in range(NT):
                        cols = slice(P * t, P * t + P)
                        for k in range(KC):
                            last = split3(bank[t][:, 0:QKV], xh[:, k, cols], xl[:, k, cols],
                                          w3h[:, k, :], w3l[:, k, :], start=(k == 0), stop=(k == KC - 1))
                        last.then_inc(qkv_ready, 1)

                def stacks(b):
                    for t in range(NT):
                        pe.wait_ge(lo_done, PRIMED + 2 * NT * b + 2 * t + 2)
                    pe.wait_ge(rot_ab, 3 * NT * (b + 1))
                    for j in range(12):
                        if j >= 4:
                            pe.wait_ge(stack_act if j % 2 == 0 else stack_dve, 6 * b + (j - 4) // 2 + 1)
                        for t in range(NT):
                            if j % 3 == 0:
                                src = ktok[:, t, j // 3, :, :].rearrange("p a s -> p (a s)")
                            else:
                                pair = 2 * (j // 3) + j % 3 - 1
                                src = qtok[:, t, 2 * pair:2 * pair + 2, :].rearrange("p a s -> p (a s)")
                            last = pe.transpose(bank[j % 4][:, P * t:P * t + P], src, ident[:, :])
                        last.then_inc(stack_ready, 1)

                def scores(b, g, i):
                    v = UNITS_S * g + i
                    if v == 0:
                        pe.wait_ge(stack_act, 6 * b + 6)
                        pe.wait_ge(stack_dve, 6 * b + 6)
                    if v >= 3:
                        pe.wait_ge(smax_done, KV * UNITS_S * b + v - 2)
                    acc = s_bank[v % 3]
                    j, heads = score_units()[i]
                    keys = P * (j + 1)
                    for a, h in enumerate(heads):
                        rows = slice(ST * (h % 2), ST * (h % 2) + ST)
                        pe.matmul(acc[:, keys * a:keys * a + keys],
                                  qst[rows, 2 * g + h // 2, P * j:P * j + P], kst[rows, g, 0:keys],
                                  start=(a == 0), stop=False, skip_group_check=True)
                    for a in range(len(heads)):
                        last = pe.matmul(acc[:, keys * (a + 1) - P:keys * (a + 1)], ident_b[:, :], causal_b[:, :],
                                         start=False, stop=(a == len(heads) - 1), skip_group_check=True)
                    last.then_inc(s_ready, 1)

                def maxima(b, g):
                    pe.wait_ge(ml_done, PRIMED + KV * b + g + 1)
                    pe.wait_ge(mT_done, PRIMED + KV * b + g)
                    pe.wait_ge(y_done, PRIMED + KV * b)
                    for j in range(NT):
                        last = pe.transpose(m_bank[0:8, P * j:P * j + P],
                                            mpart[:, g % 2, j, :, :, :].rearrange("p a b c -> p (a b c)"), ident[:, :])
                    last.then_inc(mT_ready, 1)

                def shifted(b, g, i):
                    w = UNITS_P * g + i
                    if i == 0:
                        pe.wait_ge(m_rows[g % 2], 16 * PRIMED + 16 * 4 * (2 * b + g // 2 + 1))
                    if w >= 3:
                        pe.wait_ge(exp_done, KV * UNITS_P * b + w - 2)
                    blocks = prob_units()[i]
                    for a, (h, kt, col) in enumerate(blocks):
                        rows = slice(ST * (h % 2), ST * (h % 2) + ST)
                        n = T - P * kt
                        last = pe.matmul(p_bank[w % 3][:, col:col + n],
                                         kst[rows, g, P * kt:P * kt + P], qst[rows, 2 * g + h // 2, P * kt:T],
                                         start=(a == 0), stop=(a == len(blocks) - 1), skip_group_check=True)
                    last.then_inc(p_ready, 1)

                def values(b, g, kt):
                    if kt == 0:
                        pe.wait_ge(sel_done, 4 * (KV * b + g + 1))
                        pe.wait_ge(o_done, PRIMED + KV * b + g)
                    for h in range(4):
                        u, col = prob_place(h, kt, kt)
                        last = pe.matmul(pv_bank[VW * h:VW * h + VW, P * kt:T], vtok[:, kt, g, :],
                                         pT[:, g % 2, u, col:col + T - P * kt], start=(kt == 0), stop=(kt == NT - 1))
                    if kt == NT - 1:
                        last.then_inc(pv_done, 1)

                def outputs(b, g):
                    pe.wait_ge(o_done, PRIMED + KV * b + g + 1)
                    pe.wait_ge(mT_done, PRIMED + KV * b + KV)
                    pe.wait_ge(y_done, PRIMED + KV * b + g)
                    for j in range(NT):
                        last = pe.transpose(m_bank[:, P * j:P * j + P], o_sb[:, P * j:P * j + P], ident[:, :])
                    last.then_inc(oT_ready, 1)

                def project(b):
                    pe.wait_ge(y_done, PRIMED + KV * b + KV)
                    pe.wait_ge(smax_done, KV * UNITS_S * (b + 1))
                    for k in range(KC):
                        for t in range(NT):
                            last = pe.transpose(bank[k][:, P * t:P * t + P], ytok[:, t, P * k:P * k + P], ident[:, :])
                        last.then_inc(yT_ready, 1)
                    pe.wait_ge(yl_done, PRIMED + KC * b + KC)
                    for t in range(NT):
                        cols = slice(P * t, P * t + P)
                        for k in range(KC):
                            last = split3(bank[2 + t // 2][:, C * (t % 2):C * (t % 2) + C], yh[:, k, cols], yl[:, k, cols],
                                          wph[:, k, :], wpl[:, k, :], start=(k == 0), stop=(k == KC - 1))
                        if t % 2:
                            last.then_inc(proj_ready, 1)

                def batch(b, following):
                    qkv(b)
                    stacks(b)
                    for slot in range(KV + 3):
                        for i in range(UNITS_S):
                            if slot < KV:
                                scores(b, slot, i)
                            if i == 2 and 1 <= slot <= KV:
                                maxima(b, slot - 1)
                            if i == 6 and 0 <= slot - 4 < KV:
                                outputs(b, slot - 4)
                            if 0 <= slot - 2 < KV and i < UNITS_P:
                                shifted(b, slot - 2, i)
                            if 0 <= slot - 3 < KV and i % 3 == 2:
                                values(b, slot - 3, i // 3)
                    outputs(b, KV - 1)
                    pe.wait_ge(exp_done, KV * UNITS_P * (b + 1))
                    transpose_x(b + B + 1)
                    project(b)

                pe.wait_ge(h_done, PRIMED + HT * B)
                pe.wait_ge(const_b, 3)
                pe.wait_ge(w3l_done, 2)
                pe.wait_ge(pads, 5)
                loop(pe, batch)

            for s in primed["pe"]:
                pe.sem_inc(s, PRIMED)
            transpose_weights()
            transpose_x(0)
            pe.wait_ge(wTl_done, 9)
            ffn(0, 0)
            attention()
            pe.wait_ge(yl_done, PRIMED + KC * B)
            pe.wait_ge(x_done, PRIMED + 2 * B * X_PER_CHUNK)
            ffn(B, 2)

        @block.vector
        def _(dve):
            def row_stats(n, c):
                for t in range(NT):
                    dve.bn_stats(stats[:, t, :], X[:, tiles(c, t, 1), :].rearrange("p a c -> p (a c)")).then_inc(stats_done, 1)
                dve.wait_ge(rstd_done, n)
                dve.wait_ge(stats_done, NT * n + NT)
                dve.sem_inc(dve_turn, 1)
                for t in range(NT):
                    dve.bn_aggr(mv[:, t, :], stats[:, t, :]).then_inc(mv_done, 1)
                dve.wait_ge(sum_done, 2 * n)
                dve.sem_inc(dve_turn, 1)
                dve.tensor_reduce(part_sum[:, :, :], X[:, tiles(c, 0, NT), :].rearrange("p t (a k) -> p t a k", k=16),
                                  AX.X, ALU.add).then_inc(sum_done, 1)
                dve.wait_ge(sum_done, 2 * n + 1)
                dve.tensor_reduce(row_sum[:, :], part_sum[:, :, :], AX.X, ALU.add).then_inc(sum_done, 1)

            def normalize(n, c):
                dve.wait_ge(rstd_done, n + 1)
                dve.wait_ge(xT_ready, KC * n)
                for t in range(NT):
                    dve.tensor_scalar(xn[:, t, :], X[:, tiles(c, t, 1), :].rearrange("p a c -> p (a c)"),
                                      mean[:, t:t + 1], rstd[:, t:t + 1], ALU.subtract, ALU.mult).then_inc(xn_done, 1)

            def low_x(n):
                for k in range(KC):
                    dve.wait_ge(xh_done, KC * n + k + 1)
                    dve.tensor_tensor(xl[:, k, :], tr_bank[k][:, :], xh[:, k, :].bitcast(F32), ALU.subtract).then_inc(xl_done, 1)

            def prepare():
                dve.wait_ge(w_in, 16 * (W_DMAS - 1))
                dve.tensor_scalar(wf[:, :, :], wi[:, :, :], 128.0, None, ALU.subtract).then_inc(wf_ready, 1)
                dve.tensor_scalar(wdf[:, :, :], wdi[:, :, :], 128.0, None, ALU.subtract).then_inc(wf_ready, 1)
                dve.tensor_scalar(sd_half[:, :], sd_raw[:, :], 0.5, None, ALU.mult).then_inc(wf_ready, 1)
                dve.wait_ge(x0_in, 16)
                row_stats(0, 0)
                n = 0
                for k in range(KC):
                    for first in range(0, 2 * FULL + 1, 4):
                        a, b = P * first, min(P * (first + 4), 2 * HID)
                        dve.wait_ge(wTh_done, n + 1)
                        dve.tensor_tensor(gul[:, k, a:b], gu_bank[n % 4][:, 0:b - a], guh[:, k, a:b].bitcast(F32),
                                          ALU.subtract).then_inc(wTl_done, 1)
                        n += 1
                normalize(0, 0)
                for kt in range(0, HT, 2):
                    dve.wait_ge(wTh_done, n + 1)
                    if kt + 1 < FULL:
                        dve.tensor_tensor(dl[:, kt:kt + 2, :].rearrange("p a c -> p (a c)"), gu_bank[n % 4][:, :],
                                          dh[:, kt:kt + 2, :].rearrange("p a c -> p (a c)").bitcast(F32),
                                          ALU.subtract).then_inc(wTl_done, 1)
                    else:
                        dve.tensor_tensor(dl[:, kt, :], gu_bank[n % 4][:, 0:C], dh[:, kt, :].bitcast(F32), ALU.subtract)
                        dve.tensor_tensor(dl[0:REST, kt + 1, :], gu_bank[n % 4][0:REST, C:2 * C],
                                          dh[0:REST, kt + 1, :].bitcast(F32), ALU.subtract).then_inc(wTl_done, 1)
                    n += 1
                low_x(0)

            def ffn(base, stage):
                def hidden(n, i):
                    rows = P if i < FULL else REST
                    dve.wait_ge(silu_done, HT * n + i + 1)
                    if i < FULL:
                        dve.wait_ge(up_ready, FULL * n + i + 1)
                    dve.wait_ge(hl_done, PRIMED + HT * n + max(i - 1, 0))
                    u, s = ((2 * i + 1) % 4, FULL + 1 + i) if i < FULL else (2 * i % 4, FULL)
                    dve.scalar_tensor_tensor(hf[0:rows, i % 2, :], gu_bank[u][0:rows, :], s_gu[0:rows, s:s + 1],
                                             sg[0:rows, i % 2, :], ALU.mult, ALU.mult).then_inc(h_done, 1)

                def add_down(n, c, done):
                    dve.wait_ge(down_done, PRIMED + HT * n + HT)
                    for p in range(2):
                        dve.wait_ge(x_done, PRIMED + done + p)
                        dve.tensor_tensor(delta[:, :, :], down_bank[p][:, :].rearrange("p (a c) -> p a c", a=2),
                                          sd_half[:, :].rearrange("p (a c) -> p a c", a=1).to_broadcast([P, 2, C]),
                                          ALU.mult).then_inc(delta_done, 1)
                        dve.wait_ge(delta_done, 2 * n + p + 1)
                        rows = X[:, tiles(c, 2 * p, 2), :]
                        dve.tensor_tensor(rows, rows, delta[:, :, :], ALU.add).then_inc(x_done, 1)

                def chunk(c, following):
                    n = c + base
                    nx = c + stage * B + 1
                    hidden(n, 0)
                    if following is not None:
                        row_stats(nx, following)
                    hidden(n, 1)
                    hidden(n, 2)
                    if following is not None:
                        normalize(nx, following)
                    for i in range(3, HT):
                        hidden(n, i)
                    if following is not None:
                        low_x(nx)
                    add_down(n, c, X_PER_CHUNK * (c + stage * B))

                if stage == 0:
                    loop(dve, chunk)
                else:
                    with dve.Fori(0, B - 1) as c:
                        chunk(c, c + 1)
                    chunk(B - 1, None)

            def attention():
                def rotary(b, t):
                    s = t % 2
                    qk = bank[t][:, 0:QK].rearrange("p (h d) -> p h d", d=HD)
                    dve.wait_ge(v_done, NT * b + t + 1)
                    dve.wait_ge(rot_done, PRIMED + NT * b + max(t - 1, 0))

                    def table(which, a, z):
                        return cs[:, t, which, a:z].rearrange("p (a d) -> p a d", a=1).to_broadcast([P, ROT, z - a])
                    half = HD // 2
                    dve.tensor_tensor(rot_a[:, s, :, :], qk, table(0, 0, HD), ALU.mult).then_inc(rot_ab, 1)
                    dve.tensor_tensor(rot_b[:, s, :, 0:half], qk[:, :, half:HD], table(1, 0, half), ALU.mult).then_inc(rot_ab, 1)
                    dve.tensor_tensor(rot_b[:, s, :, half:HD], qk[:, :, 0:half], table(1, half, HD), ALU.mult).then_inc(rot_ab, 1)

                def copy_stack(b, j):
                    dve.wait_ge(stack_ready, 12 * b + j + 1)
                    dst = kst[:, j // 3, :] if j % 3 == 0 else qst[:, 2 * (j // 3) + j % 3 - 1, :]
                    dve.tensor_copy(dst, bank[j % 4][:, :]).then_inc(stack_dve, 1)

                def row_max(b, g, i):
                    v = UNITS_S * g + i
                    j, heads = score_units()[i]
                    keys = P * (j + 1)
                    if i == 0:
                        dve.wait_ge(ml_done, PRIMED + KV * b + max(g - 1, 0))
                    dve.wait_ge(s_ready, KV * UNITS_S * b + v + 1)
                    dst = mneg[:, g % 2, j, heads[0]:heads[-1] + 1:2] if len(heads) == 2 else \
                        mneg[:, g % 2, j, heads[0]:heads[0] + 1]
                    dve.tensor_reduce(dst, s_bank[v % 3][:, 0:keys * len(heads)].rearrange("p (a k) -> p a k", k=keys),
                                      AX.X, ALU.max, negate=True).then_inc(smax_done, 1)

                def split_max(b, g):
                    dve.wait_ge(smax_done, KV * UNITS_S * b + UNITS_S * (g + 1))
                    dve.wait_ge(mT_ready, PRIMED + KV * b + max(g - 1, 0))
                    src = mneg[:, g % 2, :, :].rearrange("p j (pair half) -> p j half pair", half=2)
                    for half in range(2):
                        dve.tensor_copy(mpart[:, g % 2, :, half, :, 0].bitcast(F32R), src[:, :, half, :]).then_inc(mh_done, 1)
                    for half in range(2):
                        dve.wait_ge(mh_done, 2 * KV * b + 2 * g + 1 + half)
                        last = dve.tensor_tensor(mpart[:, g % 2, :, half, :, 1], src[:, :, half, :],
                                                 mpart[:, g % 2, :, half, :, 0], ALU.subtract)
                    last.then_inc(ml_done, 1)

                def copy_max(b, g):
                    dve.wait_ge(mT_ready, PRIMED + KV * b + g + 1)
                    dve.wait_ge(m_rows[g % 2], 16 * PRIMED + 16 * 4 * (2 * b + g // 2))
                    dve.tensor_copy(mT[:, g % 2, :], m_bank[0:8, :]).then_inc(mT_done, 1)

                def heads_out(b, g):
                    dve.wait_ge(oT_ready, KV * b + g + 1)
                    dve.wait_ge(y_done, PRIMED + KV * b + g)
                    o = m_bank[:, :].rearrange("p (j h d) -> p j h d", j=NT, h=4)
                    dve.reciprocal(rec[:, :], m_bank[:, HD:512:VW]).then_inc(rec_done, 1)
                    dve.wait_ge(rec_done, KV * b + g + 1)
                    inv = rec[:, :].rearrange("p (j h a) -> p j h a", j=NT, a=1).to_broadcast([P, NT, 4, HD])
                    dst = ytok[:, :, 64 * g:64 * g + 64].rearrange("p j (h d) -> p j h d", h=4)
                    dve.tensor_tensor(dst, o[:, :, :, 0:HD], inv, ALU.mult).then_inc(y_done, 1)

                def batch(b, following):
                    n = b + B + 1
                    for t in range(NT):
                        rotary(b, t)
                    for j in range(1, 12, 2):
                        copy_stack(b, j)
                    for slot in range(KV + 4):
                        for i in range(UNITS_S):
                            if slot < KV:
                                row_max(b, slot, i)
                            if i == 9 and 0 <= slot - 4 < KV:
                                heads_out(b, slot - 4)
                            if i == 5 and 1 <= slot <= KV:
                                copy_max(b, slot - 1)
                        if slot < KV:
                            split_max(b, slot)
                        if slot == 4:
                            row_stats(n, following)
                        if slot == 5:
                            normalize(n, following)
                    low_x(n)
                    for k in range(KC):
                        dve.wait_ge(yh_done, KC * b + k + 1)
                        dve.tensor_tensor(yl[:, k, :], bank[k][:, :], yh[:, k, :].bitcast(F32), ALU.subtract).then_inc(yl_done, 1)
                    for p in range(2):
                        dve.wait_ge(proj_ready, 2 * b + p + 1)
                        rows = X[:, tiles(b, 2 * p, 2), :]
                        dve.tensor_tensor(rows, bank[2 + p][:, :].rearrange("p (a c) -> p a c", a=2), rows,
                                          ALU.add).then_inc(x_done, 1)

                dve.wait_ge(c_in, 16 * C_DMAS)
                loop(dve, batch)

            for s in primed["dve"]:
                dve.sem_inc(s, PRIMED)
            prepare()
            dve.wait_ge(x_in, 16)
            dve.wait_ge(w_in, 16 * (W_DMAS - 1))
            dve.wait_ge(wf_ready, 3)
            ffn(0, 0)
            attention()
            ffn(B, 2)

        @block.scalar
        def _(act):
            def high_x(n):
                for k in range(KC):
                    act.wait_ge(xT_ready, KC * n + k + 1)
                    act.activation(xh[:, k, :], tr_bank[k][:, :], ACT.Copy).then_inc(xh_done, 1)

            def prepare():
                n = 0
                for k in range(KC):
                    for first in range(0, 2 * FULL + 1, 4):
                        a, b = P * first, min(P * (first + 4), 2 * HID)
                        act.wait_ge(wT_ready, n + 1)
                        act.activation(guh[:, k, a:b], gu_bank[n % 4][:, 0:b - a], ACT.Copy).then_inc(wTh_done, 1)
                        n += 1
                for kt in range(0, HT, 2):
                    act.wait_ge(wT_ready, n + 1)
                    if kt + 1 < FULL:
                        act.activation(dh[:, kt:kt + 2, :].rearrange("p a c -> p (a c)"), gu_bank[n % 4][:, :],
                                       ACT.Copy).then_inc(wTh_done, 1)
                    else:
                        act.activation(dh[:, kt, :], gu_bank[n % 4][:, 0:C], ACT.Copy).then_inc(w3h_done, 1)
                        act.activation(dh[0:REST, kt + 1, :], gu_bank[n % 4][0:REST, C:2 * C], ACT.Copy).then_inc(w3h_done, 1)
                        act.wait_ge(w3h_done, 2)
                        act.wait_ge(const, 5)
                        act.activation(ez[:, :], neg_half[:, 0:1], ACT.Copy).then_inc(wTh_done, 1)
                    n += 1
                high_x(0)
                act.wait_ge(c_in, 16 * C_DMAS)
                act.activation(w3h[:, :, :], w3[:, :, :], ACT.Copy).then_inc(w3h_done, 1)
                act.activation(wph[:, :, :], wp[:, :, :], ACT.Copy).then_inc(w3h_done, 1)

            def ffn(base, stage):
                def silu(n, i):
                    rows = slice(0, P) if i < FULL else slice(REST, P)
                    m = i if i < FULL else FULL
                    act.wait_ge(gate_ready, HT * n + i + 1)
                    act.wait_ge(h_done, PRIMED + HT * n + max(i - 1, 0))
                    act.activation(sg[0:P - rows.start, i % 2, :], gu_bank[2 * i % 4][rows, :], ACT.Silu,
                                   scale=s_gu[rows, m:m + 1]).then_inc(silu_done, 1)

                def high_h(n, i):
                    rows = P if i < FULL else REST
                    act.wait_ge(h_done, PRIMED + HT * n + i + 1)
                    if i == 0:
                        act.wait_ge(down_done, PRIMED + HT * n)
                    act.activation(hh[0:rows, i, :], hf[0:rows, i % 2, :], ACT.Copy).then_inc(hh_done, 1)

                def chunk(c, following):
                    n = c + base
                    silu(n, 0)
                    for i in range(1, HT):
                        silu(n, i)
                        high_h(n, i - 1)
                    high_h(n, HT - 1)
                    if following is not None:
                        high_x(c + stage * B + 1)

                if stage == 0:
                    loop(act, chunk)
                else:
                    with act.Fori(0, B - 1) as c:
                        chunk(c, c + 1)
                    chunk(B - 1, None)

            def attention():
                def copy_outputs(b, g):
                    act.wait_ge(pv_done, PRIMED + KV * b + g + 1)
                    act.wait_ge(oT_ready, KV * b + g) if g else act.wait_ge(yl_done, PRIMED + KC * b)
                    act.activation(o_sb[:, :], pv_bank[:, :], ACT.Copy).then_inc(o_done, 1)

                def batch(b, following):
                    for t in range(NT):
                        act.wait_ge(qkv_ready, NT * b + t + 1)
                        act.activation(vtok[:, t, :, 0:HD], bank[t][:, QK:QKV].rearrange("p (g d) -> p g d", d=HD),
                                       ACT.Copy).then_inc(v_done, 1)
                    for t in range(NT):
                        s = t % 2
                        act.wait_ge(rot_done, PRIMED + NT * b + t + 1)
                        q = rot[:, s, 0:HEADS, :].rearrange("p h (a d) -> p h a d", a=1).to_broadcast([P, HEADS, 2, HD])
                        qd = qtok[:, t, :, :].rearrange("p h (a d) -> p h a d", a=4)[:, :, 0::2, :][:, :, 0:2, :]
                        for a in (0, 2):
                            act.activation(qtok[:, t, :, HD * a:HD * a + HD].bitcast(F32R), rot[:, s, 0:HEADS, :],
                                           ACT.Copy).then_inc(hi_done, 1)
                        for half in range(2):
                            for a in range(2):
                                act.activation(ktok[:, t, :, half, HD * a:HD * a + HD].bitcast(F32R), rot[:, s, HEADS:, :],
                                               ACT.Copy).then_inc(hi_done, 1)
                    for j in range(0, 12, 2):
                        act.wait_ge(stack_ready, 12 * b + j + 1)
                        dst = kst[:, j // 3, :] if j % 3 == 0 else qst[:, 2 * (j // 3) + j % 3 - 1, :]
                        act.activation(dst, bank[j % 4][:, :], ACT.Copy).then_inc(stack_act, 1)
                    for g in range(KV + 1):
                        for i in range(UNITS_P):
                            if i == 3 and g >= 2:
                                copy_outputs(b, g - 2)
                            if g == KV:
                                continue
                            w = UNITS_P * g + i
                            act.wait_ge(p_ready, KV * UNITS_P * b + w + 1)
                            if i == 0:
                                act.wait_ge(pv_done, PRIMED + KV * b + max(g - 1, 0))
                            act.activation(pT[:, g % 2, i, :], p_bank[w % 3][:, :], ACT.Exp,
                                           scale=float(HD) ** -0.5).then_inc(exp_done, 1)
                    copy_outputs(b, KV - 1)
                    high_x(b + B + 1)
                    for k in range(KC):
                        act.wait_ge(yT_ready, KC * b + k + 1)
                        act.activation(yh[:, k, :], bank[k][:, :], ACT.Copy).then_inc(yh_done, 1)

                loop(act, batch)

            ez = sg[:, 0, 0:1]
            for s in primed["act"]:
                act.sem_inc(s, PRIMED)
            prepare()
            ffn(0, 0)
            attention()
            ffn(B, 2)

        @block.gpsimd
        def _(pool):
            def constants():
                pool.memset(ident[:, :], 1.0).then_inc(const, 1)
                pool.wait_ge(const, 1)
                pool.affine_select(out=ident[:, :], in_=ident[:, :], compare_op=ALU.is_equal, fill=0.0, base=0,
                                   pattern=[[1, P]], channel_multiplier=-1).then_inc(const, 1)
                pool.memset(neg_half[:, :], -0.5).then_inc(const, 1)
                pool.memset(inv_c[:, :], 1.0 / C).then_inc(const, 1)
                pool.memset(eps[:, :], EPS).then_inc(const, 1)
                pool.memset(causal_b[:, :], 0.0).then_inc(const_b, 1)
                pool.wait_ge(const, 2)
                pool.tensor_copy(ident_b[:, :], ident[:, :]).then_inc(const_b, 1)
                pool.wait_ge(const_b, 1)
                pool.affine_select(out=causal_b[:, :], in_=causal_b[:, :], compare_op=ALU.is_ge, fill=NEG, base=0,
                                   pattern=[[-1, P]], channel_multiplier=1).then_inc(const_b, 1)

            def padding():
                pool.memset(qtok[:, :, :, 3 * HD:], 0.0).then_inc(pads, 1)
                pool.memset(ktok[:, :, :, :, 3 * HD + 2:], 0.0).then_inc(pads, 1)
                pool.memset(ktok[:, :, :, :, 3 * HD:3 * HD + 2], 1.0).then_inc(pads, 1)
                pool.memset(vtok[:, :, :, HD:HD + 1], 1.0).then_inc(pads, 1)
                pool.memset(vtok[:, :, :, HD + 1:], 0.0).then_inc(pads, 1)

            def deviation(n):
                pool.wait_ge(mv_done, NT * n + NT)
                pool.wait_ge(xn_done, NT * n)
                pool.wait_ge(sum_done, 2 * n + 2)
                pool.tensor_tensor(mean[:, :], row_sum[:, :], inv_c[:, :], ALU.mult).then_inc(veps_done, 1)
                pool.tensor_tensor(veps[:, :], mv[:, :, 1], eps[:, :], ALU.add).then_inc(veps_done, 1)
                pool.wait_ge(veps_done, 2 * n + 2)
                pool.tensor_tensor(rstd[:, :], veps[:, :], neg_half[:, :], ALU.pow).then_inc(rstd_done, 1)

            def split_projections():
                pool.wait_ge(w3h_done, 3)
                pool.tensor_tensor(w3l[:, :, :], w3[:, :, :], w3h[:, :, :].bitcast(F32), ALU.subtract).then_inc(w3l_done, 1)
                pool.wait_ge(w3h_done, 4)
                pool.tensor_tensor(wpl[:, :, :], wp[:, :, :], wph[:, :, :].bitcast(F32), ALU.subtract).then_inc(w3l_done, 1)

            def ffn(base, stage):
                def low_h(n, i):
                    rows = P if i < FULL else REST
                    pool.wait_ge(hh_done, HT * n + i + 1)
                    pool.tensor_tensor(hl[0:rows, i, :], hf[0:rows, i % 2, :], hh[0:rows, i, :].bitcast(F32),
                                       ALU.subtract).then_inc(hl_done, 1)

                def chunk(c, following):
                    for i in range(HT):
                        low_h(c + base, i)
                        if i == 0 and following is not None:
                            deviation(c + stage * B + 1)

                if stage == 0:
                    loop(pool, chunk)
                else:
                    with pool.Fori(0, B - 1) as c:
                        chunk(c, c + 1)
                    chunk(B - 1, None)

            def attention():
                def wait_exp(count):
                    pool.wait_ge(exp_done, count)
                    pool.sem_inc(pool_turn, 1)

                def mask(g, first, count, col, step):
                    units = pT[:, g % 2, first:UNITS_P, :].rearrange("p u n -> p (u n)")
                    view = units.rearrange("p (a n) -> p a n", n=step)[:, 0:count, col:col + P]
                    pool.affine_select(out=view, in_=view, compare_op=ALU.is_ge, fill=0.0, base=0,
                                       pattern=[[0, count], [1, P]], channel_multiplier=-1).then_inc(sel_done, 1)

                def batch(b, following):
                    for t in range(NT):
                        s = t % 2
                        pool.wait_ge(rot_ab, 3 * (NT * b + t + 1))
                        pool.wait_ge(hi_done, PRIMED + 6 * (NT * b + max(t - 1, 0)))
                        pool.wait_ge(lo_done, PRIMED + 2 * (NT * b + max(t - 1, 0)))
                        pool.tensor_tensor(rot[:, s, :, :], rot_a[:, s, :, :], rot_b[:, s, :, :], ALU.add).then_inc(rot_done, 1)
                        pool.wait_ge(hi_done, PRIMED + 6 * (NT * b + t + 1))
                        pool.tensor_tensor(qtok[:, t, :, HD:2 * HD], rot[:, s, 0:HEADS, :], qtok[:, t, :, 0:HD],
                                           ALU.subtract).then_inc(lo_done, 1)
                        k_src = rot[:, s, HEADS:, :]
                        pool.tensor_tensor(ktok[:, t, :, 0, 2 * HD:3 * HD], k_src, ktok[:, t, :, 0, 0:HD], ALU.subtract)
                        pool.tensor_tensor(ktok[:, t, :, 1, 2 * HD:3 * HD], k_src, ktok[:, t, :, 1, 0:HD],
                                           ALU.subtract).then_inc(lo_done, 1)
                    for g in range(KV):
                        exps = KV * UNITS_P * b + UNITS_P * g
                        wait_exp(exps + 4)
                        mask(g, 0, 4, 0, 512)
                        wait_exp(exps + 8)
                        mask(g, 4, 4, 0, 512)
                        mask(g, 4, 4, 384, 512)
                        wait_exp(exps + 10)
                        mask(g, 8, 4, 0, 256)
                        if g == 2:
                            deviation(b + B + 1)

                loop(pool, batch)

            for s in primed["pool"]:
                pool.sem_inc(s, PRIMED)
            constants()
            pool.wait_ge(const, 5)
            deviation(0)
            padding()
            split_projections()
            ffn(0, 0)
            attention()
            ffn(B, 2)


def rope_tables():
    import numpy as np
    inv = (np.float32(1.0) / np.float32(10000.0) ** (np.arange(0, HD, 2, dtype=np.float32) / np.float32(HD))).astype(np.float32)
    angle = (np.arange(T, dtype=np.float32)[:, None] * inv[None, :]).astype(np.float32)
    cos, sin = np.cos(angle), np.sin(angle)
    table = np.stack([np.concatenate([cos, cos], 1), np.concatenate([-sin, sin], 1)], 1)
    return np.ascontiguousarray(table.reshape(NT, P, 2, HD).transpose(1, 0, 2, 3)).astype(np.float32)


_INS = ["L0_attn_x", "L0_attn_Wq", "L0_attn_Wk", "L0_attn_Wv", "L0_attn_Wproj", "L0_ffn_wq_gate", "L0_ffn_s_gate",
        "L0_ffn_wq_up", "L0_ffn_s_up", "L0_ffn_wq_down", "L0_ffn_s_down"]


def kernel(**inputs):
    import numpy as np
    import concourse.bacc as bacc
    from concourse.bass_utils import run_bass_kernel_spmd as run

    nc = bacc.Bacc("TRN2", target_bir_lowering=False, num_devices=1)
    arrays = {f"{n}_dram": np.ascontiguousarray(inputs[n]) for n in _INS}
    arrays["rope_dram"] = rope_tables()
    args = [nc.dram_tensor(n, a.shape, mybir.dt.from_np(a.dtype), kind="ExternalInput").ap() for n, a in arrays.items()]
    out = nc.dram_tensor("out_dram", (B, T, C), F32, kind="ExternalOutput").ap()
    build(nc, *args, out)
    return run(nc, [arrays], core_ids=[0]).results[0]["out_dram"]
```

```python
from contextlib import ExitStack

import concourse.bass as bass
from concourse import mybir

F32 = mybir.dt.float32
F32R = mybir.dt.float32r
BF16 = mybir.dt.bfloat16
I32 = mybir.dt.int32
ACT = mybir.ActivationFunctionType
ALU = mybir.AluOpType
AX = mybir.AxisListType

P = 128
B, T, C = 4, 512, 256
HEADS, KV, HD = 16, 4, 16
HID = 704
NT = T // P
KC = C // P
FULL = HID // P
REST = HID - FULL * P
HT = FULL + 1
QKV = C + 2 * KV * HD
QK = C + KV * HD
ROT = HEADS + KV
ST = 64
UNITS_S = 12
UNITS_P = 10
VW = 32
PASSES = 3
NEG = -3.0e38
EPS = 1e-5


def score_units():
    units = [(0, (0, 2)), (0, (1, 3)), (1, (0, 2)), (1, (1, 3))]
    return units + [(j, (h,)) for j in (2, 3) for h in range(4)]


def prob_units():
    return ([[(h, 0, 0)] for h in range(4)] + [[(h, 1, 0), (h, 3, 384)] for h in range(4)]
            + [[(h, 2, 0), (h + 2, 2, 256)] for h in range(2)])


def prob_place(h, kt, j):
    if kt == 0:
        return h, P * j
    if kt == 1:
        return 4 + h, P * (j - 1)
    if kt == 3:
        return 4 + h, 384
    return 8 + h % 2, 256 * (h // 2) + P * (j - 2)


QKV_AT = [(2, 3), (2, 6), (2, 9), (3, 0)]


JOBS = {(slot, i): ("stack", slot + 1, i) for slot in range(KV - 1) for i in range(3)}
JOBS.update({(KV - 1, (4, 5, 6)[i]): ("stack", KV, i) for i in range(3)})
JOBS.update({(1, 5 + k): ("x", k) for k in range(KC)})
JOBS.update({step: ("qkv", t) for t, step in enumerate(QKV_AT)})
JOBS.update({(3, 7 + k): ("y", k) for k in range(KC)})
JOBS.update({(3, 10 + p): ("proj", p) for p in range(2)})
VALUES_AT = [3, 5, 7, 9]
OUTPUTS_AT, HEADS_AT = 5, 6
HIGH_AT = [(2, 5), (2, 8), (2, 11), (3, 2)]
LOW_AT = [(2, 6), (2, 9), (3, 0), (3, 3)]
STATS_AT, DEVIATION_AT, NORMALIZE_AT = (0, 5), (0, 8), (1, 1)
STEPS = [(slot, i) for slot in range(KV) for i in range(UNITS_S)]
RING = [key for step in STEPS for key in ([JOBS[step]] if step in JOBS else []) + [("s",) + step]]


def live(b, g):
    return not isinstance(b, int) or 0 <= KV * b + g < KV * B


def present(key, b):
    if not isinstance(b, int):
        return True
    if key[0] == "s":
        return 0 <= b < B
    if key[0] == "stack":
        return live(b, key[1])
    if key[0] == "x":
        return 0 <= b < B
    if key[0] == "qkv":
        return 0 <= b + 1 < B
    return 0 <= b - 1 < B


def build(nc, x, wq, wk, wv, wproj, w_gate, s_gate, w_up, s_up, w_down, s_down, rope, out):
    with ExitStack() as ctx:
        def sb(name, shape, dt=F32):
            return ctx.enter_context(nc.sbuf_tensor(name, shape, dt))

        def sem(name):
            return ctx.enter_context(nc.semaphore(name))

        bank = [ctx.enter_context(nc.psum_tensor(f"bank{i}", [P, 512], F32)) for i in range(8)]
        gu_bank = bank[0:4]
        tr_bank = bank[4:6]
        down_bank = bank[6:8]
        s_bank = bank[0:3]
        p_bank = bank[3:6]
        pv_bank, m_bank = bank[6], bank[7]

        X = sb("X", [P, B * NT, C])
        xn = sb("xn", [P, NT, C])
        stats = sb("stats", [P, NT, 6])
        mv = sb("mv", [P, NT, 2])
        part_sum = sb("part_sum", [P, NT, 16])
        row_sum = sb("row_sum", [P, NT])
        mean = sb("mean", [P, NT])
        inv_c = sb("inv_c", [P, NT])
        veps = sb("veps", [P, NT])
        rstd = sb("rstd", [P, NT])
        neg_half = sb("neg_half", [P, NT])
        eps = sb("eps", [P, NT])
        xh = sb("xh", [P, KC, T], F32R)
        xl = sb("xl", [P, KC, T], F32R)
        ident = sb("ident", [P, P])
        ident_r = sb("ident_r", [P, P], F32R)
        ident_b = sb("ident_b", [P, P], BF16)
        causal_b = sb("causal_b", [P, 2, P], BF16)

        pT = sb("pT", [P, 2, UNITS_P, 512])
        raw = pT[:, :, :, :].rearrange("p a u n -> p (a u n)")
        n_gu, n_d = (2 * FULL + 1) * C, KC * HID
        wi = raw[:, 0:n_gu].bitcast(I32).rearrange("p (m c) -> p m c", c=C)
        wf = raw[:, n_gu:2 * n_gu].rearrange("p (m c) -> p m c", c=C)
        wdi = raw[:, 2 * n_gu:2 * n_gu + n_d].bitcast(I32).rearrange("p (m c) -> p m c", c=HID)
        wdf = raw[:, 2 * n_gu + n_d:2 * (n_gu + n_d)].rearrange("p (m c) -> p m c", c=HID)
        n_end = 2 * (n_gu + n_d)
        guh = sb("guh", [P, KC, 2 * HID], F32R)
        gul = sb("gul", [P, KC, 2 * HID], F32R)
        dh = sb("dh", [P, HT, C], F32R)
        dl = sb("dl", [P, HT, C], F32R)
        s_gu = sb("s_gu", [P, 2 * FULL + 1])
        sd_raw = raw[:, n_end + KC * QKV + KC * C:n_end + KC * QKV + KC * C + C]
        sd_half = sb("sd_half", [P, C])
        w3 = raw[:, n_end:n_end + KC * QKV].rearrange("p (k n) -> p k n", n=QKV)
        w3h = sb("w3h", [P, KC, QKV], F32R)
        w3l = sb("w3l", [P, KC, QKV], F32R)
        wp = raw[:, n_end + KC * QKV:n_end + KC * QKV + KC * C].rearrange("p (k n) -> p k n", n=C)
        wph = sb("wph", [P, KC, C], F32R)
        wpl = sb("wpl", [P, KC, C], F32R)
        cs = sb("cs", [P, NT, 2, HD])

        sg = sb("sg", [P, 2, T])
        hf = sb("hf", [P, 2, T])
        hh = sb("hh", [P, HT, T], F32R)
        hl = sb("hl", [P, HT, T], F32R)
        delta = sb("delta", [P, 2, C])

        def idle(buffer):
            return buffer[:, :, 0:ROT * HD].rearrange("p s (h d) -> p s h d", d=HD)
        rot_a = idle(sg)
        rot_b = hf[:, 1, 0:ROT * HD].rearrange("p (h d) -> p h d", d=HD)
        rot = sb("rot", [P, 2, ROT, HD])
        qtok = sb("qtok", [P, NT, HEADS, ST], F32R)
        ktok = sb("ktok", [P, NT, KV, 2, ST], F32R)
        v_new = delta[:, :, :].rearrange("p a (t g d) -> p (a t) g d", t=NT, g=KV)[:, 0:NT, :, :]
        v_mid = delta[:, :, :].rearrange("p a (t g d) -> p (a t) g d", t=NT, g=KV)[:, NT:, :, :]
        vtok = sb("vtok", [P, NT, KV, VW])
        qst = sb("qst", [P, HEADS // 2, T], F32R)
        kst = sb("kst", [P, KV, T], F32R)
        mneg = sb("mneg", [P, 2, NT, 4])
        mpad = [sb(f"mpart{i}", [P, NT * 8 + P - 8], F32R) for i in range(2)]
        mpart = [m[:, 0:NT * 8].rearrange("p (j half pair part) -> p j half pair part", j=NT, half=2, pair=2) for m in mpad]
        mT = hl[0:8, KC:KC + 2, :]
        rec = sb("rec", [P, 16])
        o_sb = hf[:, 0, :]
        low_parts = mneg[:, 0, 0, :]
        low_rows = mneg[:, 0, 1, 0:1]
        low_most = mneg[0:1, 0, 2, 0:1]
        low_flag = rec[0:1, 0:1].bitcast(I32)
        ytok = sb("ytok", [P, NT, C])
        yh, yl = hh[:, 0:KC, :], hl[:, 0:KC, :]

        x0_in, x_in, w_in, c_in = sem("x0_in"), sem("x_in"), sem("w_in"), sem("c_in")
        const = sem("const")
        const_b = sem("const_b")
        pads = sem("pads")
        wf_ready = sem("wf_ready")
        wT_ready, wTh_done, wTl_done = sem("wT_ready"), sem("wTh_done"), sem("wTl_done")
        w3h_done, w3l_done = sem("w3h_done"), sem("w3l_done")
        stats_done, mv_done, veps_done, rstd_done = (sem(n) for n in ("stats_done", "mv_done", "veps_done", "rstd_done"))
        xn_done, xT_ready, xh_done, xl_done = (sem(n) for n in ("xn_done", "xT_ready", "xh_done", "xl_done"))
        gate_ready, up_ready, silu_done = sem("gate_ready"), sem("up_ready"), sem("silu_done")
        h_done, hh_done, hl_done, down_done = (sem(n) for n in ("h_done", "hh_done", "hl_done", "down_done"))
        delta_done, x_done = sem("delta_done"), sem("x_done")
        qkv_ready, v_done, rot_ab, rot_done = (sem(n) for n in ("qkv_ready", "v_done", "rot_ab", "rot_done"))
        hi_done, lo_done = sem("hi_done"), sem("lo_done")
        stack_ready, stack_done = sem("stack_ready"), sem("stack_done")
        s_ready, smax_done = sem("s_ready"), sem("smax_done")
        mh_done, ml_done, mT_ready, mT_done = (sem(n) for n in ("mh_done", "ml_done", "mT_ready", "mT_done"))
        m_rows = [sem("m_rows0"), sem("m_rows1")]
        p_ready, exp_done, sel_done, pv_done = (sem(n) for n in ("p_ready", "exp_done", "sel_done", "pv_done"))
        o_done, oT_ready, rec_done, y_done = (sem(n) for n in ("o_done", "oT_ready", "rec_done", "y_done"))
        yT_ready, yh_done, yl_done, proj_ready = (sem(n) for n in ("yT_ready", "yh_done", "yl_done", "proj_ready"))
        stored = sem("stored")
        low_read, low_rows_done, low_row_ready, low_flag_done = (
            sem(n) for n in ("low_read", "low_rows_done", "low_row_ready", "low_flag_done"))
        v_moved, v_in = sem("v_moved"), sem("v_in")
        sum_done = sem("sum_done")
        dve_turn, pool_turn = sem("dve_turn"), sem("pool_turn")

        x_rows = x.rearrange("b (t p) c -> p (b t) c", p=P)
        out_rows = out.rearrange("b (t p) c -> p (b t) c", p=P)
        W_DMAS = 4 + 2 + 4 + 1
        C_DMAS = 5
        PRIMED = 1
        primed = dict(pe=[down_done, mT_ready, pv_done], dve=[h_done, x_done, yl_done, y_done, ml_done, rot_done],
                      act=[hi_done, o_done, mT_done], pool=[hl_done, lo_done])
        PADS = 7

        def ring_bank(key):
            return bank[RING.index(key) % 3]

        def read_done(key):
            kind, a = key[0], key[1:]
            if kind == "s":
                return smax_done, KV * UNITS_S, UNITS_S * a[0] + a[1] + 1
            if kind == "stack":
                return stack_done, 3 * KV, 3 * a[0] + a[1] + 1
            if kind == "x":
                return xl_done, KC, KC * (B + 1) + a[0] + 1
            if kind == "qkv":
                return rot_ab, 3 * NT, 3 * (NT + a[0] + 1)
            if kind == "y":
                return yl_done, KC, PRIMED - KC + a[0] + 1
            return x_done, X_PER_CHUNK, PRIMED + X_PER_CHUNK * (B - 1) + a[0] + 1

        X_PER_CHUNK = 2

        def tiles(c, first, count):
            return bass.ds(c * NT + first, count)

        def loop(eng, body):
            with eng.Fori(0, B - 1) as c:
                body(c, c + 1)
            body(B - 1, 0)

        def pipeline(eng, iteration):
            iteration(-1)
            iteration(0)
            with eng.Fori(1, B - 1) as b:
                iteration(b)
            iteration(B - 1)
            iteration(B)

        block = ctx.enter_context(nc.Block())

        @block.sync
        def _(sp):
            sp.dma_start(X[:, 0:NT, :], x_rows[:, 0:NT, :]).then_inc(x0_in, 16)
            sp.dma_start(wi[:, 0:FULL, :], w_gate[0:FULL * P, :].rearrange("(m p) c -> p m c", p=P)).then_inc(w_in, 16)
            sp.dma_start(wi[REST:P, FULL, :], w_gate[FULL * P:HID, :]).then_inc(w_in, 16)
            sp.dma_start(wi[0:REST, FULL, :], w_up[FULL * P:HID, :]).then_inc(w_in, 16)
            sp.dma_start(wi[:, FULL + 1:, :], w_up[0:FULL * P, :].rearrange("(m p) c -> p m c", p=P)).then_inc(w_in, 16)
            sp.dma_start(wdi[:, :, :], w_down.rearrange("(m p) h -> p m h", p=P)).then_inc(w_in, 16)
            sp.dma_start(sd_raw[:, :], s_down.rearrange("(a c) -> a c", a=1).to_broadcast([P, C])).then_inc(w_in, 16)
            with nc.allow_non_contiguous_dma("scales, one per hidden row"):
                sp.dma_start(s_gu[:, 0:FULL], s_gate[0:FULL * P].rearrange("(m p) -> p m", p=P)).then_inc(w_in, 16)
                sp.dma_start(s_gu[REST:P, FULL:FULL + 1], s_gate[FULL * P:HID].rearrange("(p a) -> p a", a=1)).then_inc(w_in, 16)
                sp.dma_start(s_gu[0:REST, FULL:FULL + 1], s_up[FULL * P:HID].rearrange("(p a) -> p a", a=1)).then_inc(w_in, 16)
                sp.dma_start(s_gu[:, FULL + 1:], s_up[0:FULL * P].rearrange("(m p) -> p m", p=P)).then_inc(w_in, 16)
            sp.dma_start(X[:, NT:, :], x_rows[:, NT:, :]).then_inc(x_in, 16)
            sp.dma_start(w3[:, :, 0:C], wq.rearrange("(k p) n -> p k n", p=P)).then_inc(c_in, 16)
            sp.dma_start(w3[:, :, C:QK], wk.rearrange("(k p) n -> p k n", p=P)).then_inc(c_in, 16)
            sp.dma_start(w3[:, :, QK:QKV], wv.rearrange("(k p) n -> p k n", p=P)).then_inc(c_in, 16)
            sp.dma_start(wp[:, :, :], wproj.rearrange("(k p) n -> p k n", p=P)).then_inc(c_in, 16)
            sp.dma_start(cs[:, :, :, :], rope).then_inc(c_in, 16)

            for s in m_rows:
                sp.sem_inc(s, 16 * PRIMED)

            def batch(b):
                for g in range(KV):
                    sp.wait_ge(mT_done, PRIMED + KV * b + g + 1)
                    for half in range(2):
                        for pair in range(2):
                            row = ST * half + 3 * HD
                            src = 4 * half + 2 * pair
                            sp.dma_start(qst[row:row + 2, 2 * g + pair, :].bitcast(F32),
                                         mT[src:src + 2, g % 2, :].bitcast(F32)).then_inc(m_rows[g % 2], 16)

            with sp.Fori(0, B) as b:
                batch(b)

            with sp.Fori(0, B) as c:
                sp.wait_ge(x_done, PRIMED + 2 * B * X_PER_CHUNK + X_PER_CHUNK * (c + 1))
                sp.dma_start(out_rows[:, tiles(c, 0, NT), :], X[:, tiles(c, 0, NT), :]).then_inc(stored, 16)
            sp.wait_ge(stored, 16 * B)

        @block.tensor
        def _(pe):
            def split3(acc, ah, al, bh, bl, start, stop, check=False):
                pe.matmul(acc, ah, bh, start=start, stop=False, skip_group_check=check)
                if bl is not None:
                    last = pe.matmul(acc, ah, bl, start=False, stop=(stop and al is None), skip_group_check=check)
                if al is not None:
                    last = pe.matmul(acc, al, bh, start=False, stop=stop, skip_group_check=check)
                return last

            def transpose_weights():
                pe.wait_ge(const, 2)
                n = 0
                for k in range(KC):
                    for first in range(0, 2 * FULL + 1, 4):
                        pe.wait_ge(wf_ready, 1)
                        if n >= 4:
                            pe.wait_ge(wTl_done, n - 3)
                        width = min(4, 2 * FULL + 1 - first)
                        for m in range(width):
                            last = pe.transpose(gu_bank[n % 4][:, P * m:P * m + P],
                                                wf[:, first + m, P * k:P * k + P], ident[:, :])
                        last.then_inc(wT_ready, 1)
                        n += 1
                pe.wait_ge(wf_ready, 2)
                for kt in range(0, HT, 2):
                    pe.wait_ge(wTl_done, n - 3)
                    for i in range(2):
                        for m in range(KC):
                            rows = P if kt + i < FULL else REST
                            last = pe.transpose(gu_bank[n % 4][0:rows, C * i + P * m:C * i + P * m + P],
                                                wdf[:, m, P * (kt + i):P * (kt + i) + rows], ident[:, :])
                    last.then_inc(wT_ready, 1)
                    n += 1

            def transpose_x(n, banks=tr_bank):
                pe.wait_ge(xn_done, NT * n + NT)
                pe.wait_ge(xl_done, KC * n)
                for k in range(KC):
                    for t in range(NT):
                        last = pe.transpose(banks[k][:, P * t:P * t + P], xn[:, t, P * k:P * k + P], ident[:, :])
                    last.then_inc(xT_ready, 1)

            def hidden(n, acc, m, low):
                for k in range(KC):
                    cols = slice(P * m, P * m + P)
                    last = split3(acc, guh[:, k, cols], gul[:, k, cols] if low else None, xh[:, k, :], xl[:, k, :],
                                  start=(k == 0), stop=(k == KC - 1))
                return last

            def gate_up(n, i, low):
                pe.wait_ge(h_done, PRIMED + HT * n + max(i - 1, 0))
                if i < FULL:
                    hidden(n, gu_bank[2 * i % 4][:, :], i, low).then_inc(gate_ready, 1)
                    hidden(n, gu_bank[(2 * i + 1) % 4][:, :], FULL + 1 + i, low).then_inc(up_ready, 1)
                else:
                    hidden(n, gu_bank[2 * i % 4][:, :], FULL, low).then_inc(gate_ready, 1)

            def down(n, kt, low):
                pe.wait_ge(hl_done, PRIMED + HT * n + kt + 1)
                rows = P if kt < FULL else REST
                for t in range(NT):
                    cols = slice(P * t, P * t + P)
                    last = split3(down_bank[t // 2][:, C * (t % 2):C * (t % 2) + C],
                                  hh[0:rows, kt, cols], hl[0:rows, kt, cols], dh[0:rows, kt, :],
                                  dl[0:rows, kt, :] if low else None,
                                  start=(kt == 0 and t % 2 == 0), stop=(kt == HT - 1), check=True)
                last.then_inc(down_done, 1)

            def chunk(stage, c, following, low, first=False):
                n = c + (B if stage else 0)
                pe.wait_ge(xl_done, KC * (c + stage * B) + KC)
                gate_up(n, 0, low)
                gate_up(n, 1, low)
                gate_up(n, 2, low)
                pe.wait_ge(x_done, PRIMED + X_PER_CHUNK * (c + stage * B))
                down(n, 0, low)
                gate_up(n, 3, low)
                down(n, 1, low)
                gate_up(n, 4, low)
                down(n, 2, low)
                gate_up(n, 5, low)
                if first:
                    pe.wait_ge(low_rows_done, 1)
                    pe.transpose(gu_bank[3][0:1, 0:P], low_rows[:, :], ident[:, :]).then_inc(low_row_ready, 1)
                if following is not None:
                    transpose_x(c + stage * B + 1)
                for kt in range(3, HT):
                    down(n, kt, low)

            def chunks(stage, low):
                with pe.Fori(0 if stage else 1, B - 1) as c:
                    chunk(stage, c, c + 1, low)
                chunk(stage, B - 1, None if stage else 0, low)

            def ffn(stage, any_low):
                with pe.If(any_low):
                    chunks(stage, True)
                with pe.Else():
                    chunks(stage, False)

            def attention():
                def take_bank(key, b):
                    at = RING.index(key)
                    for i in range(at - 3, -1, -3):
                        if present(RING[i], b):
                            done, per, offset = read_done(RING[i])
                            pe.wait_ge(done, per * b + offset)
                            return
                    if isinstance(b, int) and b < 0:
                        return
                    for i in range(len(RING) - 1, -1, -1):
                        if i % 3 == at % 3 and present(RING[i], b - 1 if isinstance(b, int) else b):
                            done, per, offset = read_done(RING[i])
                            pe.wait_ge(done, per * b + offset - per)
                            return

                def qkv(b, t):
                    if t == 0:
                        pe.wait_ge(xl_done, KC * b + KC * (B + 2))
                    cols = slice(P * t, P * t + P)
                    for k in range(KC):
                        last = split3(ring_bank(("qkv", t))[:, 0:QKV], xh[:, k, cols], xl[:, k, cols],
                                      w3h[:, k, :], w3l[:, k, :], start=(k == 0), stop=(k == KC - 1))
                    last.then_inc(qkv_ready, 1)

                def stack(b, g, j):
                    if g == KV:
                        pe.wait_ge(lo_done, PRIMED + 2 * NT * 2 + 2 * NT * b)
                    for t in range(NT):
                        if j == 0:
                            src = ktok[:, t, g % KV, :, :].rearrange("p a s -> p (a s)")
                        else:
                            first = 4 * (g % KV) + 2 * (j - 1)
                            src = qtok[:, t, first:first + 2, :].rearrange("p a s -> p (a s)")
                        last = pe.transpose(ring_bank(("stack", g, j))[:, P * t:P * t + P], src.bitcast(F32), ident[:, :])
                    last.then_inc(stack_ready, 1)

                def transposes(src, acc, k, ready):
                    for t in range(NT):
                        last = pe.transpose(acc[:, P * t:P * t + P], src[:, t, P * k:P * k + P], ident[:, :])
                    last.then_inc(ready, 1)

                def project(b, p):
                    if p == 0:
                        pe.wait_ge(yl_done, PRIMED + KC * b)
                    acc = ring_bank(("proj", p))
                    for t in (2 * p, 2 * p + 1):
                        cols = slice(P * t, P * t + P)
                        for k in range(KC):
                            last = split3(acc[:, C * (t % 2):C * (t % 2) + C], yh[:, k, cols], yl[:, k, cols],
                                          wph[:, k, :], wpl[:, k, :], start=(k == 0), stop=(k == KC - 1))
                    last.then_inc(proj_ready, 1)

                def job(b, key):
                    take_bank(key, b)
                    if key[0] == "stack":
                        stack(b, key[1], key[2])
                    elif key[0] == "x":
                        if key[1] == 0:
                            pe.wait_ge(xn_done, NT * b + NT * (B + 2))
                        transposes(xn, ring_bank(key), key[1], xT_ready)
                    elif key[0] == "qkv":
                        qkv(b, key[1])
                    elif key[0] == "y":
                        if key[1] == 0:
                            pe.wait_ge(y_done, PRIMED + KV * b)
                        transposes(ytok, ring_bank(key), key[1], yT_ready)
                    else:
                        project(b, key[1])

                def scores(b, g, i):
                    if i == 0:
                        pe.wait_ge(stack_done, 3 * KV * b + 3 * (g + 1))
                    take_bank(("s", g, i), b)
                    acc = ring_bank(("s", g, i))
                    j, heads = score_units()[i]
                    keys = P * (j + 1)
                    n = len(heads)
                    for a, h in enumerate(heads):
                        rows = slice(ST * (h % 2), ST * (h % 2) + ST)
                        pe.matmul(acc[:, keys * a:keys * a + keys],
                                  qst[rows, 2 * g + h // 2, P * j:P * j + P], kst[rows, g, 0:keys],
                                  start=(a == 0), stop=False, skip_group_check=True)
                    diagonal = acc[:, 0:keys * n].rearrange("p (a k) -> p a k", k=keys)[:, :, keys - P:keys]
                    pe.matmul(diagonal, ident_b[:, :], causal_b[:, 0:n, :], start=False, stop=True,
                              skip_group_check=True).then_inc(s_ready, 1)

                def maxima(b, g):
                    pe.wait_ge(ml_done, PRIMED + KV * b + g + 1)
                    if live(b, g - 4):
                        pe.wait_ge(y_done, PRIMED + KV * b + g - 3)
                    elif live(b, g - 1):
                        pe.wait_ge(mT_done, PRIMED + KV * b + g)
                    for j in range(NT):
                        last = pe.transpose(m_bank[:, P * j:P * j + P], mpad[g % 2][:, 8 * j:8 * j + P].bitcast(F32), ident[:, :])
                    last.then_inc(mT_ready, 1)

                def shifted(b, g, i):
                    w = UNITS_P * (g + 2) + i
                    if i == 0:
                        pe.wait_ge(m_rows[g % 2], 16 * 4 * 2 * b + 16 * (PRIMED + 4 * (g // 2 + 1)))
                    if live(b, g - 1) or i >= 3:
                        pe.wait_ge(exp_done, KV * UNITS_P * b + UNITS_P * g + i - (2 if w else 0))
                    blocks = prob_units()[i]
                    for a, (h, kt, col) in enumerate(blocks):
                        rows = slice(ST * (h % 2), ST * (h % 2) + ST)
                        n = T - P * kt
                        last = pe.matmul(p_bank[w % 3][:, col:col + n],
                                         kst[rows, g % KV, P * kt:P * kt + P], qst[rows, 2 * (g % KV) + h // 2, P * kt:T],
                                         start=(a == 0), stop=(a == len(blocks) - 1), skip_group_check=True)
                    last.then_inc(p_ready, 1)

                def values(b, g, kt):
                    if kt == 0:
                        pe.wait_ge(sel_done, 4 * KV * b + 4 * (g + 1))
                        pe.wait_ge(o_done, PRIMED + KV * b + g)
                        pe.wait_ge(v_in, KV * b + g + 1)
                    for h in range(4):
                        u, col = prob_place(h, kt, kt)
                        last = pe.matmul(pv_bank[VW * h:VW * h + VW, P * kt:T], vtok[:, kt, g % KV, :],
                                         pT[:, g % 2, u, col:col + T - P * kt], start=(kt == 0), stop=(kt == NT - 1))
                    if kt == NT - 1:
                        last.then_inc(pv_done, 1)

                def outputs(b, g):
                    pe.wait_ge(o_done, PRIMED + KV * b + g + 1)
                    if live(b, g + 3):
                        pe.wait_ge(mT_done, PRIMED + KV * b + g + 4)
                    else:
                        pe.wait_ge(y_done, PRIMED + KV * b + g)
                    for j in range(NT):
                        last = pe.transpose(m_bank[:, P * j:P * j + P], o_sb[:, P * j:P * j + P], ident[:, :])
                    last.then_inc(oT_ready, 1)

                def iteration(b):
                    for slot, i in STEPS:
                        key = JOBS.get((slot, i))
                        if key and present(key, b):
                            job(b, key)
                        if live(b, slot) and present(("s",), b):
                            scores(b, slot, i)
                        if i == 2 and live(b, slot - 1):
                            maxima(b, slot - 1)
                        if i == OUTPUTS_AT and live(b, slot - 4):
                            outputs(b, slot - 4)
                        if i < UNITS_P and live(b, slot - 2):
                            shifted(b, slot - 2, i)
                        if i in VALUES_AT and live(b, slot - 3):
                            values(b, slot - 3, VALUES_AT.index(i))

                pe.wait_ge(h_done, PRIMED + HT * B)
                pe.wait_ge(const_b, 4)
                pe.wait_ge(w3l_done, 2)
                pe.wait_ge(pads, PADS)
                pe.wait_ge(x_done, PRIMED + X_PER_CHUNK * B)
                pipeline(pe, iteration)

            for s in primed["pe"]:
                pe.sem_inc(s, PRIMED)
            transpose_weights()
            transpose_x(0)
            pe.wait_ge(wTl_done, 9)
            chunk(0, 0, 1, True, first=True)
            pe.wait_ge(low_flag_done, 1)
            any_low = pe.value_load(low_flag[0:1, 0:1], min_val=0, max_val=1)
            ffn(0, any_low)
            attention()
            pe.wait_ge(x_done, PRIMED + 2 * X_PER_CHUNK * B)
            ffn(2, any_low)

        @block.vector
        def _(dve):
            def row_stats(n, c):
                for t in range(NT):
                    dve.bn_stats(stats[:, t, :], X[:, tiles(c, t, 1), :].rearrange("p a c -> p (a c)")).then_inc(stats_done, 1)
                dve.wait_ge(rstd_done, n)
                dve.wait_ge(stats_done, NT * n + NT)
                dve.sem_inc(dve_turn, 1)
                for t in range(NT):
                    dve.bn_aggr(mv[:, t, :], stats[:, t, :]).then_inc(mv_done, 1)
                dve.wait_ge(sum_done, 2 * n)
                dve.sem_inc(dve_turn, 1)
                dve.tensor_reduce(part_sum[:, :, :], X[:, tiles(c, 0, NT), :].rearrange("p t (a k) -> p t a k", k=16),
                                  AX.X, ALU.add).then_inc(sum_done, 1)
                dve.wait_ge(sum_done, 2 * n + 1)
                dve.tensor_reduce(row_sum[:, :], part_sum[:, :, :], AX.X, ALU.add).then_inc(sum_done, 1)

            def normalize(n, c):
                dve.wait_ge(rstd_done, n + 1)
                dve.wait_ge(xT_ready, KC * n)
                for t in range(NT):
                    dve.tensor_scalar(xn[:, t, :], X[:, tiles(c, t, 1), :].rearrange("p a c -> p (a c)"),
                                      mean[:, t:t + 1], rstd[:, t:t + 1], ALU.subtract, ALU.mult).then_inc(xn_done, 1)

            def low_x(n, banks=tr_bank):
                for k in range(KC):
                    dve.wait_ge(xh_done, KC * n + k + 1)
                    dve.tensor_tensor(xl[:, k, :], banks[k][:, :], xh[:, k, :].bitcast(F32), ALU.subtract).then_inc(xl_done, 1)

            def prepare():
                dve.wait_ge(w_in, 16 * (W_DMAS - 1))
                dve.tensor_scalar(wf[:, :, :], wi[:, :, :], 128.0, None, ALU.subtract).then_inc(wf_ready, 1)
                dve.tensor_scalar(wdf[:, :, :], wdi[:, :, :], 128.0, None, ALU.subtract).then_inc(wf_ready, 1)
                dve.tensor_scalar(sd_half[:, :], sd_raw[:, :], 0.5, None, ALU.mult).then_inc(wf_ready, 1)
                dve.wait_ge(x0_in, 16)
                row_stats(0, 0)
                n = 0
                for k in range(KC):
                    for first in range(0, 2 * FULL + 1, 4):
                        a, b = P * first, min(P * (first + 4), 2 * HID)
                        dve.wait_ge(wTh_done, n + 1)
                        dve.tensor_tensor(gul[:, k, a:b], gu_bank[n % 4][:, 0:b - a], guh[:, k, a:b].bitcast(F32),
                                          ALU.subtract).then_inc(wTl_done, 1)
                        n += 1
                normalize(0, 0)
                for kt in range(0, HT, 2):
                    dve.wait_ge(wTh_done, n + 1)
                    if kt + 1 < FULL:
                        dve.tensor_tensor(dl[:, kt:kt + 2, :].rearrange("p a c -> p (a c)"), gu_bank[n % 4][:, :],
                                          dh[:, kt:kt + 2, :].rearrange("p a c -> p (a c)").bitcast(F32),
                                          ALU.subtract).then_inc(wTl_done, 1)
                    else:
                        dve.tensor_tensor(dl[:, kt, :], gu_bank[n % 4][:, 0:C], dh[:, kt, :].bitcast(F32), ALU.subtract)
                        dve.tensor_tensor(dl[0:REST, kt + 1, :], gu_bank[n % 4][0:REST, C:2 * C],
                                          dh[0:REST, kt + 1, :].bitcast(F32), ALU.subtract).then_inc(wTl_done, 1)
                    n += 1
                low_x(0)

            def ffn(base, stage):
                def hidden(n, i):
                    rows = P if i < FULL else REST
                    dve.wait_ge(silu_done, HT * n + i + 1)
                    if i < FULL:
                        dve.wait_ge(up_ready, FULL * n + i + 1)
                    dve.wait_ge(hl_done, PRIMED + HT * n + max(i - 1, 0))
                    u, s = ((2 * i + 1) % 4, FULL + 1 + i) if i < FULL else (2 * i % 4, FULL)
                    dve.scalar_tensor_tensor(hf[0:rows, i % 2, :], gu_bank[u][0:rows, :], s_gu[0:rows, s:s + 1],
                                             sg[0:rows, i % 2, :], ALU.mult, ALU.mult).then_inc(h_done, 1)

                def add_down(n, c, done):
                    dve.wait_ge(down_done, PRIMED + HT * n + HT)
                    for p in range(2):
                        dve.wait_ge(x_done, PRIMED + done + p)
                        dve.tensor_tensor(delta[:, :, :], down_bank[p][:, :].rearrange("p (a c) -> p a c", a=2),
                                          sd_half[:, :].rearrange("p (a c) -> p a c", a=1).to_broadcast([P, 2, C]),
                                          ALU.mult).then_inc(delta_done, 1)
                        dve.wait_ge(delta_done, 2 * n + p + 1)
                        rows = X[:, tiles(c, 2 * p, 2), :]
                        dve.tensor_tensor(rows, rows, delta[:, :, :], ALU.add).then_inc(x_done, 1)

                def largest_low(i, low, rows=P):
                    dve.tensor_reduce(low_parts[0:rows, i:i + 1], low, AX.X, ALU.max, apply_absolute_value=True).then_inc(low_read, 1)

                def chunk(c, following, first=False):
                    n = c + base
                    nx = c + stage * B + 1
                    hidden(n, 0)
                    if following is not None:
                        row_stats(nx, following)
                    hidden(n, 1)
                    if first:
                        largest_low(0, gul[:, 0, :].bitcast(F32))
                    hidden(n, 2)
                    if first:
                        largest_low(1, gul[:, 1, :].bitcast(F32))
                    if following is not None:
                        normalize(nx, following)
                    hidden(n, 3)
                    if first:
                        largest_low(2, dl[:, 0:FULL, :].rearrange("p m c -> p (m c)").bitcast(F32))
                        largest_low(3, dl[0:REST, FULL, :].bitcast(F32), REST)
                        dve.wait_ge(low_read, 4)
                        dve.tensor_reduce(low_rows[:, :], low_parts[:, :], AX.X, ALU.max).then_inc(low_rows_done, 1)
                    hidden(n, 4)
                    hidden(n, 5)
                    if first:
                        dve.wait_ge(low_row_ready, 1)
                        dve.tensor_reduce(low_most[:, :], gu_bank[3][0:1, 0:P], AX.X, ALU.max).then_inc(low_read, 1)
                        dve.wait_ge(low_read, 5)
                        dve.tensor_scalar(low_flag[:, :], low_most[:, :], 0.0, None, ALU.is_gt).then_inc(low_flag_done, 1)
                    if following is not None:
                        low_x(nx)
                    add_down(n, c, X_PER_CHUNK * (c + stage * B))

                if stage == 0:
                    chunk(0, 1, first=True)
                    with dve.Fori(1, B - 1) as c:
                        chunk(c, c + 1)
                    chunk(B - 1, 0)
                else:
                    with dve.Fori(0, B - 1) as c:
                        chunk(c, c + 1)
                    chunk(B - 1, None)

            def attention():
                def rotary(b, t):
                    s = t % 2
                    n = NT * b + NT + t
                    qk = ring_bank(("qkv", t))[:, 0:QK].rearrange("p (h d) -> p h d", d=HD)
                    dve.wait_ge(v_done, n + 1)
                    dve.wait_ge(rot_done, n + PRIMED)

                    def table(which, a, z):
                        return cs[:, t, which, a:z].rearrange("p (a d) -> p a d", a=1).to_broadcast([P, ROT, z - a])
                    half = HD // 2
                    dve.tensor_tensor(rot_a[:, s, :, :], qk, table(0, 0, HD), ALU.mult).then_inc(rot_ab, 1)
                    dve.tensor_tensor(rot_b[:, :, 0:half], qk[:, :, half:HD], table(1, 0, half), ALU.mult).then_inc(rot_ab, 1)
                    dve.tensor_tensor(rot_b[:, :, half:HD], qk[:, :, 0:half], table(1, half, HD), ALU.mult).then_inc(rot_ab, 1)
                    dve.wait_ge(rot_ab, 3 * n + 3)
                    before = NT * b + NT + max(t - 1, 0)
                    dve.wait_ge(hi_done, 6 * before + PRIMED)
                    dve.wait_ge(lo_done, 2 * before + PRIMED)
                    dve.tensor_tensor(rot[:, s, :, :], rot_a[:, s, :, :], rot_b[:, :, :], ALU.add).then_inc(rot_done, 1)

                def row_max(b, g, i):
                    j, heads = score_units()[i]
                    keys = P * (j + 1)
                    if i == 0 and live(b, g - 1):
                        dve.wait_ge(ml_done, PRIMED + KV * b + g)
                    dve.wait_ge(s_ready, KV * UNITS_S * b + UNITS_S * g + i + 1)
                    dst = mneg[:, g % 2, j, heads[0]:heads[-1] + 1:2] if len(heads) == 2 else \
                        mneg[:, g % 2, j, heads[0]:heads[0] + 1]
                    acc = ring_bank(("s", g, i))
                    dve.tensor_reduce(dst, acc[:, 0:keys * len(heads)].rearrange("p (a k) -> p a k", k=keys),
                                      AX.X, ALU.max, negate=True).then_inc(smax_done, 1)

                def split_max(b, g):
                    dve.wait_ge(smax_done, KV * UNITS_S * b + UNITS_S * (g + 1))
                    if live(b, g - 1):
                        dve.wait_ge(mT_ready, PRIMED + KV * b + g - 1 + (g == 0))
                    src = mneg[:, g % 2, :, :].rearrange("p j (pair half) -> p j half pair", half=2)
                    for half in range(2):
                        dve.tensor_copy(mpart[g % 2][:, :, half, :, 0], src[:, :, half, :]).then_inc(mh_done, 1)
                    for half in range(2):
                        dve.wait_ge(mh_done, 2 * KV * b + 2 * g + 1 + half)
                        last = dve.tensor_tensor(mpart[g % 2][:, :, half, :, 1], src[:, :, half, :],
                                                 mpart[g % 2][:, :, half, :, 0].bitcast(F32), ALU.subtract)
                    last.then_inc(ml_done, 1)

                def heads_out(b, g):
                    dve.wait_ge(oT_ready, KV * b + g - KV + 1)
                    dve.wait_ge(y_done, PRIMED + KV * b + g - KV)
                    o = m_bank[:, :].rearrange("p (j h d) -> p j h d", j=NT, h=4)
                    dve.reciprocal(rec[:, :], m_bank[:, HD:512:VW]).then_inc(rec_done, 1)
                    dve.wait_ge(rec_done, KV * b + g - KV + 1)
                    inv = rec[:, :].rearrange("p (j h a) -> p j h a", j=NT, a=1).to_broadcast([P, NT, 4, HD])
                    dst = ytok[:, :, 64 * g:64 * g + 64].rearrange("p j (h d) -> p j h d", h=4)
                    dve.tensor_tensor(dst, o[:, :, :, 0:HD], inv, ALU.mult).then_inc(y_done, 1)

                def read_job(b, key):
                    kind, at = key[0], key[1]
                    if kind == "x":
                        dve.wait_ge(xh_done, KC * b + KC * (B + 1) + at + 1)
                        dve.tensor_tensor(xl[:, at, :], ring_bank(key)[:, :], xh[:, at, :].bitcast(F32),
                                          ALU.subtract).then_inc(xl_done, 1)
                    elif kind == "qkv":
                        rotary(b, at)
                    elif kind == "y":
                        dve.wait_ge(yh_done, KC * b - KC + at + 1)
                        dve.tensor_tensor(yl[:, at, :], ring_bank(key)[:, :], yh[:, at, :].bitcast(F32),
                                          ALU.subtract).then_inc(yl_done, 1)
                    elif kind == "proj":
                        dve.wait_ge(proj_ready, 2 * b - 2 + at + 1)
                        rows = X[:, tiles(b, 2 * at - NT, 2), :]
                        dve.tensor_tensor(rows, ring_bank(key)[:, :].rearrange("p (a c) -> p a c", a=2), rows,
                                          ALU.add).then_inc(x_done, 1)

                def iteration(b):
                    following = 0 if isinstance(b, int) and b == B - 1 else b + 1
                    for slot, i in STEPS:
                        if present(("s",), b):
                            row_max(b, slot, i)
                            if i == UNITS_S - 1:
                                split_max(b, slot)
                        key = JOBS.get((slot, i))
                        if key and present(key, b):
                            read_job(b, key)
                        if i == HEADS_AT and live(b, slot - 4):
                            heads_out(b, slot)
                        if present(("x",), b):
                            if (slot, i) == STATS_AT:
                                row_stats(b + B + 1, following)
                            if (slot, i) == NORMALIZE_AT:
                                normalize(b + B + 1, following)

                dve.wait_ge(c_in, 16 * C_DMAS)
                pipeline(dve, iteration)

            for s in primed["dve"]:
                dve.sem_inc(s, PRIMED)
            prepare()
            dve.wait_ge(const, 6)
            dve.wait_ge(x_in, 16)
            dve.wait_ge(w_in, 16 * (W_DMAS - 1))
            dve.wait_ge(wf_ready, 3)
            ffn(0, 0)
            attention()
            ffn(B, 2)

        @block.scalar
        def _(act):
            def high_x(n, banks=tr_bank):
                for k in range(KC):
                    act.wait_ge(xT_ready, KC * n + k + 1)
                    act.activation(xh[:, k, :], banks[k][:, :], ACT.Copy).then_inc(xh_done, 1)

            def prepare():
                n = 0
                for k in range(KC):
                    for first in range(0, 2 * FULL + 1, 4):
                        a, b = P * first, min(P * (first + 4), 2 * HID)
                        act.wait_ge(wT_ready, n + 1)
                        act.activation(guh[:, k, a:b], gu_bank[n % 4][:, 0:b - a], ACT.Copy).then_inc(wTh_done, 1)
                        n += 1
                for kt in range(0, HT, 2):
                    act.wait_ge(wT_ready, n + 1)
                    if kt + 1 < FULL:
                        act.activation(dh[:, kt:kt + 2, :].rearrange("p a c -> p (a c)"), gu_bank[n % 4][:, :],
                                       ACT.Copy).then_inc(wTh_done, 1)
                    else:
                        act.activation(dh[:, kt, :], gu_bank[n % 4][:, 0:C], ACT.Copy).then_inc(w3h_done, 1)
                        act.activation(dh[0:REST, kt + 1, :], gu_bank[n % 4][0:REST, C:2 * C], ACT.Copy).then_inc(w3h_done, 1)
                        act.wait_ge(w3h_done, 2)
                        act.wait_ge(const, 6)
                        act.activation(ez[:, :], neg_half[:, 0:1], ACT.Copy).then_inc(wTh_done, 1)
                    n += 1
                high_x(0)
                act.wait_ge(c_in, 16 * C_DMAS)
                act.activation(w3h[:, :, :], w3[:, :, :], ACT.Copy).then_inc(w3h_done, 1)
                act.activation(wph[:, :, :], wp[:, :, :], ACT.Copy).then_inc(w3h_done, 1)

            def ffn(base, stage):
                def silu(n, i):
                    rows = slice(0, P) if i < FULL else slice(REST, P)
                    m = i if i < FULL else FULL
                    act.wait_ge(gate_ready, HT * n + i + 1)
                    act.wait_ge(h_done, PRIMED + HT * n + max(i - 1, 0))
                    act.activation(sg[0:P - rows.start, i % 2, :], gu_bank[2 * i % 4][rows, :], ACT.Silu,
                                   scale=s_gu[rows, m:m + 1]).then_inc(silu_done, 1)

                def high_h(n, i):
                    rows = P if i < FULL else REST
                    act.wait_ge(h_done, PRIMED + HT * n + i + 1)
                    if i == 0:
                        act.wait_ge(down_done, PRIMED + HT * n)
                    act.activation(hh[0:rows, i, :], hf[0:rows, i % 2, :], ACT.Copy).then_inc(hh_done, 1)

                def chunk(c, following):
                    n = c + base
                    silu(n, 0)
                    for i in range(1, HT):
                        silu(n, i)
                        high_h(n, i - 1)
                    high_h(n, HT - 1)
                    if following is not None:
                        high_x(c + stage * B + 1)

                if stage == 0:
                    loop(act, chunk)
                else:
                    with act.Fori(0, B - 1) as c:
                        chunk(c, c + 1)
                    chunk(B - 1, None)

            def attention():
                def copy_outputs(b, g):
                    act.wait_ge(pv_done, PRIMED + KV * b + g + 1)
                    if live(b, g - 1):
                        act.wait_ge(oT_ready, KV * b + g)
                    act.activation(o_sb[:, :], pv_bank[:, :], ACT.Copy).then_inc(o_done, 1)

                def copy_values(b, t):
                    act.wait_ge(qkv_ready, NT * b + NT + t + 1)
                    if t == 0 and live(b, 0):
                        act.wait_ge(v_moved, b + 1)
                    act.activation(v_new[:, t, :, :], ring_bank(("qkv", t))[:, QK:QKV].rearrange("p (g d) -> p g d", d=HD),
                                   ACT.Copy).then_inc(v_done, 1)

                def high_qk(b, t):
                    s = t % 2
                    act.wait_ge(rot_done, PRIMED + NT + NT * b + t + 1)
                    for a in (0, 2):
                        act.activation(qtok[:, t, :, HD * a:HD * a + HD], rot[:, s, 0:HEADS, :], ACT.Copy).then_inc(hi_done, 1)
                    for half in range(2):
                        for a in range(2):
                            act.activation(ktok[:, t, :, half, HD * a:HD * a + HD], rot[:, s, HEADS:, :],
                                           ACT.Copy).then_inc(hi_done, 1)

                def copy_max(b, g):
                    act.wait_ge(mT_ready, PRIMED + KV * b + g + 1)
                    if live(b, g - 2):
                        act.wait_ge(m_rows[g % 2], 16 * 4 * 2 * b + 16 * (PRIMED + 4 * (g // 2)))
                    act.activation(mT[:, g % 2, :], m_bank[0:8, :], ACT.Copy).then_inc(mT_done, 1)

                def exps(b, g, i):
                    w = UNITS_P * (g + 2) + i
                    act.wait_ge(p_ready, KV * UNITS_P * b + UNITS_P * g + i + 1)
                    if i == 0 and live(b, g - 2):
                        act.wait_ge(pv_done, PRIMED + KV * b + g - 1)
                    act.activation(pT[:, g % 2, i, :], p_bank[w % 3][:, :], ACT.Exp,
                                   scale=float(HD) ** -0.5).then_inc(exp_done, 1)

                def read_job(b, key):
                    kind, at = key[0], key[1]
                    if kind == "stack":
                        g, j = key[1:]
                        act.wait_ge(stack_ready, 3 * KV * b + 3 * g + j + 1)
                        dst = kst[:, g % KV, :] if j == 0 else qst[:, 2 * (g % KV) + j - 1, :]
                        act.activation(dst, ring_bank(key)[:, :], ACT.Copy).then_inc(stack_done, 1)
                    elif kind == "x":
                        act.wait_ge(xT_ready, KC * b + KC * (B + 1) + at + 1)
                        act.activation(xh[:, at, :], ring_bank(key)[:, :], ACT.Copy).then_inc(xh_done, 1)
                    elif kind == "qkv":
                        copy_values(b, at)
                    elif kind == "y":
                        act.wait_ge(yT_ready, KC * b - KC + at + 1)
                        act.activation(yh[:, at, :], ring_bank(key)[:, :], ACT.Copy).then_inc(yh_done, 1)

                def iteration(b):
                    for slot, i in STEPS:
                        if i == 0 and live(b, slot - 4):
                            copy_outputs(b, slot - 4)
                        key = JOBS.get((slot, i))
                        if key and present(key, b):
                            read_job(b, key)
                        if (slot, i) in HIGH_AT and present(("qkv",), b):
                            high_qk(b, HIGH_AT.index((slot, i)))
                        if i < UNITS_P and live(b, slot - 2):
                            exps(b, slot - 2, i)
                        if i == 2 and live(b, slot - 1):
                            copy_max(b, slot - 1)

                pipeline(act, iteration)

            ez = sg[:, 0, 0:1]
            for s in primed["act"]:
                act.sem_inc(s, PRIMED)
            prepare()
            ffn(0, 0)
            attention()
            ffn(B, 2)

        @block.gpsimd
        def _(pool):
            def constants():
                pool.memset(ident[:, :], 1.0).then_inc(const, 1)
                pool.wait_ge(const, 1)
                pool.affine_select(out=ident[:, :], in_=ident[:, :], compare_op=ALU.is_equal, fill=0.0, base=0,
                                   pattern=[[1, P]], channel_multiplier=-1).then_inc(const, 1)
                pool.memset(low_parts[:, :], 0.0).then_inc(const, 1)
                pool.memset(neg_half[:, :], -0.5).then_inc(const, 1)
                pool.memset(inv_c[:, :], 1.0 / C).then_inc(const, 1)
                pool.memset(eps[:, :], EPS).then_inc(const, 1)
                pool.memset(causal_b[:, :, :], 0.0).then_inc(const_b, 1)
                pool.wait_ge(const, 2)
                pool.tensor_copy(ident_b[:, :], ident[:, :]).then_inc(const_b, 1)
                pool.tensor_copy(ident_r[:, :], ident[:, :]).then_inc(const_b, 1)
                pool.wait_ge(const_b, 1)
                pool.affine_select(out=causal_b[:, :, :], in_=causal_b[:, :, :], compare_op=ALU.is_ge, fill=NEG, base=0,
                                   pattern=[[0, 2], [-1, P]], channel_multiplier=1).then_inc(const_b, 1)

            def padding():
                pool.memset(qtok[:, :, :, 3 * HD:].bitcast(F32), 0.0).then_inc(pads, 1)
                pool.memset(ktok[:, :, :, :, 3 * HD + 2:].bitcast(F32), 0.0).then_inc(pads, 1)
                pool.memset(ktok[:, :, :, :, 3 * HD:3 * HD + 2].bitcast(F32), 1.0).then_inc(pads, 1)
                pool.memset(vtok[:, :, :, HD:HD + 1], 1.0).then_inc(pads, 1)
                pool.memset(vtok[:, :, :, HD + 1:], 0.0).then_inc(pads, 1)
                for m in mpad:
                    pool.memset(m[:, :].bitcast(F32), 0.0).then_inc(pads, 1)

            def deviation(n):
                pool.wait_ge(mv_done, NT * n + NT)
                pool.wait_ge(xn_done, NT * n)
                pool.wait_ge(sum_done, 2 * n + 2)
                pool.tensor_tensor(mean[:, :], row_sum[:, :], inv_c[:, :], ALU.mult).then_inc(veps_done, 1)
                pool.tensor_tensor(veps[:, :], mv[:, :, 1], eps[:, :], ALU.add).then_inc(veps_done, 1)
                pool.wait_ge(veps_done, 2 * n + 2)
                pool.tensor_tensor(rstd[:, :], veps[:, :], neg_half[:, :], ALU.pow).then_inc(rstd_done, 1)

            def split_projections():
                pool.wait_ge(w3h_done, 3)
                pool.tensor_tensor(w3l[:, :, :], w3[:, :, :], w3h[:, :, :].bitcast(F32), ALU.subtract).then_inc(w3l_done, 1)
                pool.wait_ge(w3h_done, 4)
                pool.tensor_tensor(wpl[:, :, :], wp[:, :, :], wph[:, :, :].bitcast(F32), ALU.subtract).then_inc(w3l_done, 1)

            def ffn(base, stage):
                def low_h(n, i):
                    rows = P if i < FULL else REST
                    pool.wait_ge(hh_done, HT * n + i + 1)
                    pool.tensor_tensor(hl[0:rows, i, :], hf[0:rows, i % 2, :], hh[0:rows, i, :].bitcast(F32),
                                       ALU.subtract).then_inc(hl_done, 1)

                def chunk(c, following):
                    for i in range(HT):
                        low_h(c + base, i)
                        if i == 0 and following is not None:
                            deviation(c + stage * B + 1)

                if stage == 0:
                    loop(pool, chunk)
                else:
                    with pool.Fori(0, B - 1) as c:
                        chunk(c, c + 1)
                    chunk(B - 1, None)

            def attention():
                def wait_exp(count):
                    pool.wait_ge(exp_done, count)
                    pool.sem_inc(pool_turn, 1)

                def mask(g, first, count, col, step):
                    units = pT[:, g % 2, first:UNITS_P, :].rearrange("p u n -> p (u n)")
                    view = units.rearrange("p (a n) -> p a n", n=step)[:, 0:count, col:col + P]
                    pool.affine_select(out=view, in_=view, compare_op=ALU.is_ge, fill=0.0, base=0,
                                       pattern=[[0, count], [1, P]], channel_multiplier=-1).then_inc(sel_done, 1)

                def low_qk(b, t):
                    s = t % 2
                    pool.wait_ge(hi_done, 6 * NT * b + PRIMED + 6 * (NT + t + 1))
                    pool.tensor_tensor(qtok[:, t, :, HD:2 * HD], rot[:, s, 0:HEADS, :], qtok[:, t, :, 0:HD].bitcast(F32),
                                       ALU.subtract).then_inc(lo_done, 1)
                    k_src = rot[:, s, HEADS:, :]
                    pool.tensor_tensor(ktok[:, t, :, 0, 2 * HD:3 * HD], k_src, ktok[:, t, :, 0, 0:HD].bitcast(F32), ALU.subtract)
                    pool.tensor_tensor(ktok[:, t, :, 1, 2 * HD:3 * HD], k_src, ktok[:, t, :, 1, 0:HD].bitcast(F32),
                                       ALU.subtract).then_inc(lo_done, 1)

                def move_values(b):
                    pool.wait_ge(v_done, NT * b + NT)
                    if live(b, -1):
                        pool.wait_ge(v_in, KV * b)
                    pool.sem_inc(pool_turn, 1)
                    pool.tensor_copy(v_mid[:, :, :, :], v_new[:, :, :, :]).then_inc(v_moved, 1)

                def take_values(b, g):
                    if g >= 0:
                        pool.wait_ge(v_moved, b + 1)
                    if live(b, g - 4):
                        pool.wait_ge(pv_done, PRIMED + KV * b + g - 3)
                    pool.sem_inc(pool_turn, 1)
                    pool.tensor_copy(vtok[:, :, g % KV, 0:HD], v_mid[:, :, g % KV, :]).then_inc(v_in, 1)

                def iteration(b):
                    for slot, i in STEPS:
                        if (slot, i) == (1, 0) and live(b, 0):
                            move_values(b)
                        if i == 0 and live(b, slot - 1):
                            take_values(b, slot - 1)
                        if live(b, slot - 2):
                            g = slot - 2
                            exps = KV * UNITS_P * b + UNITS_P * g
                            if i == 4:
                                wait_exp(exps + 4)
                                mask(g, 0, 4, 0, 512)
                            if i == 8:
                                wait_exp(exps + 8)
                                mask(g, 4, 4, 0, 512)
                                mask(g, 4, 4, 384, 512)
                            if i == 10:
                                wait_exp(exps + 10)
                                mask(g, 8, 4, 0, 256)
                        if (slot, i) in LOW_AT and present(("qkv",), b):
                            low_qk(b, LOW_AT.index((slot, i)))
                        if (slot, i) == DEVIATION_AT and present(("x",), b):
                            deviation(b + B + 1)

                pipeline(pool, iteration)

            for s in primed["pool"]:
                pool.sem_inc(s, PRIMED)
            constants()
            pool.wait_ge(const, 6)
            deviation(0)
            padding()
            split_projections()
            ffn(0, 0)
            attention()
            ffn(B, 2)


def rope_tables():
    import numpy as np
    inv = (np.float32(1.0) / np.float32(10000.0) ** (np.arange(0, HD, 2, dtype=np.float32) / np.float32(HD))).astype(np.float32)
    angle = (np.arange(T, dtype=np.float32)[:, None] * inv[None, :]).astype(np.float32)
    cos, sin = np.cos(angle), np.sin(angle)
    table = np.stack([np.concatenate([cos, cos], 1), np.concatenate([-sin, sin], 1)], 1)
    return np.ascontiguousarray(table.reshape(NT, P, 2, HD).transpose(1, 0, 2, 3)).astype(np.float32)


_INS = ["L0_attn_x", "L0_attn_Wq", "L0_attn_Wk", "L0_attn_Wv", "L0_attn_Wproj", "L0_ffn_wq_gate", "L0_ffn_s_gate",
        "L0_ffn_wq_up", "L0_ffn_s_up", "L0_ffn_wq_down", "L0_ffn_s_down"]


def kernel(**inputs):
    import numpy as np
    import concourse.bacc as bacc
    from concourse.bass_utils import run_bass_kernel_spmd as run

    nc = bacc.Bacc("TRN2", target_bir_lowering=False, num_devices=1)
    arrays = {f"{n}_dram": np.ascontiguousarray(inputs[n]) for n in _INS}
    arrays["rope_dram"] = rope_tables()
    args = [nc.dram_tensor(n, a.shape, mybir.dt.from_np(a.dtype), kind="ExternalInput").ap() for n, a in arrays.items()]
    out = nc.dram_tensor("out_dram", (B, T, C), F32, kind="ExternalOutput").ap()
    build(nc, *args, out)
    return run(nc, [arrays], core_ids=[0]).results[0]["out_dram"]
```

```python
from contextlib import ExitStack

import concourse.bass as bass
from concourse import mybir

F32 = mybir.dt.float32
F32R = mybir.dt.float32r
BF16 = mybir.dt.bfloat16
I32 = mybir.dt.int32
ACT = mybir.ActivationFunctionType
ALU = mybir.AluOpType
AX = mybir.AxisListType

P = 128
B, T, C = 4, 512, 256
HEADS, KV, HD = 16, 4, 16
HID = 704
NT = T // P
KC = C // P
FULL = HID // P
REST = HID - FULL * P
HT = FULL + 1
QKV = C + 2 * KV * HD
QK = C + KV * HD
ROT = HEADS + KV
ST = 64
UNITS_S = 12
UNITS_P = 10
VW = 32
NEG = -3.0e38
EPS = 1e-5


def score_units():
    units = [(0, (0, 2)), (0, (1, 3)), (1, (0, 2)), (1, (1, 3))]
    return units + [(j, (h,)) for j in (2, 3) for h in range(4)]


def prob_units():
    return ([[(h, 0, 0)] for h in range(4)] + [[(h, 1, 0), (h, 3, 384)] for h in range(4)]
            + [[(h, 2, 0), (h + 2, 2, 256)] for h in range(2)])


def prob_place(h, kt, j):
    if kt == 0:
        return h, P * j
    if kt == 1:
        return 4 + h, P * (j - 1)
    if kt == 3:
        return 4 + h, 384
    return 8 + h % 2, 256 * (h // 2) + P * (j - 2)


STEPS = [(slot, i) for slot in range(KV) for i in range(UNITS_S)]
S_BANKS, P_BANKS = 4, 2
VALUES_AT = [3, 5, 7, 9]
OUTPUTS_AT, HEADS_AT = 4, 5
STATS_AT, SUMS_AT, DEVIATION_AT, NORMALIZE_AT = (0, 4), (0, 7), (0, 9), (1, 0)
X_AT = [(1, 4), (1, 6)]
QKV_AT = [(2, 3), (2, 6), (2, 9), (3, 0)]
HIGH_AT = [(2, 5), (2, 8), (2, 11), (3, 2)]
LOW_AT = [(2, 6), (2, 9), (3, 0), (3, 3)]
STACK_AT = [[(slot, i) for i in range(3)] for slot in range(KV - 1)] + [[(3, 5), (3, 6), (3, 7)]]
Y_AT = [(3, 8), (3, 9)]
PROJ_AT = [(3, 10), (3, 11)]
JOBS = {step: ("stack", slot + 1, j) for slot in range(KV) for j, step in enumerate(STACK_AT[slot])}
for name, places in (("x", X_AT), ("qkv", QKV_AT), ("y", Y_AT), ("proj", PROJ_AT)):
    JOBS.update({step: (name, j) for j, step in enumerate(places)})
RING = [key for step in STEPS for key in ([JOBS[step]] if step in JOBS else []) + [("s",) + step]]


def live(b, g):
    return not isinstance(b, int) or 0 <= KV * b + g < KV * B


def present(key, b):
    if not isinstance(b, int):
        return True
    if key[0] == "s":
        return 0 <= b < B
    if key[0] == "stack":
        return live(b, key[1])
    if key[0] == "x":
        return 0 <= b < B
    if key[0] == "qkv":
        return 0 <= b + 1 < B
    return 0 <= b - 1 < B


def build(nc, x, wq, wk, wv, wproj, w_gate, s_gate, w_up, s_up, w_down, s_down, rope, out):
    with ExitStack() as ctx:
        def sb(name, shape, dt=F32):
            return ctx.enter_context(nc.sbuf_tensor(name, shape, dt))

        def sem(name):
            return ctx.enter_context(nc.semaphore(name))

        bank = [ctx.enter_context(nc.psum_tensor(f"bank{i}", [P, 512], F32)) for i in range(8)]
        gu_bank = bank[0:4]
        tr_bank = bank[4:6]
        down_bank = bank[6:8]
        p_bank = bank[S_BANKS:6]
        pv_bank, m_bank = bank[6], bank[7]

        X = sb("X", [P, B * NT, C])
        xn = sb("xn", [P, NT, C])
        stats = sb("stats", [P, NT, 6])
        mv = sb("mv", [P, NT, 2])
        part_sum = sb("part_sum", [P, NT, 16])
        row_sum = sb("row_sum", [P, NT])
        mean = sb("mean", [P, NT])
        inv_c = sb("inv_c", [P, NT])
        veps = sb("veps", [P, NT])
        rstd = sb("rstd", [P, NT])
        neg_half = sb("neg_half", [P, NT])
        eps = sb("eps", [P, NT])
        xh = sb("xh", [P, KC, T], F32R)
        xl = sb("xl", [P, KC, T], F32R)
        ident = sb("ident", [P, P])
        ident_b = sb("ident_b", [P, P], BF16)
        causal_b = sb("causal_b", [P, 2, P], BF16)

        pT = sb("pT", [P, 2, UNITS_P, 512])
        raw = pT[:, :, :, :].rearrange("p a u n -> p (a u n)")
        n_gu, n_d = (2 * FULL + 1) * C, KC * HID
        wi = raw[:, 0:n_gu].bitcast(I32).rearrange("p (m c) -> p m c", c=C)
        wf = raw[:, n_gu:2 * n_gu].rearrange("p (m c) -> p m c", c=C)
        wdi = raw[:, 2 * n_gu:2 * n_gu + n_d].bitcast(I32).rearrange("p (m c) -> p m c", c=HID)
        wdf = raw[:, 2 * n_gu + n_d:2 * (n_gu + n_d)].rearrange("p (m c) -> p m c", c=HID)
        n_end = 2 * (n_gu + n_d)
        guh = sb("guh", [P, KC, 2 * HID], F32R)
        gul = sb("gul", [P, KC, 2 * HID], F32R)
        dh = sb("dh", [P, HT, C], F32R)
        dl = sb("dl", [P, HT, C], F32R)
        s_gu = sb("s_gu", [P, 2 * FULL + 1])
        sd_raw = raw[:, n_end + KC * QKV + KC * C:n_end + KC * QKV + KC * C + C]
        sd_half = sb("sd_half", [P, C])
        w3 = raw[:, n_end:n_end + KC * QKV].rearrange("p (k n) -> p k n", n=QKV)
        w3h = sb("w3h", [P, KC, QKV], F32R)
        w3l = sb("w3l", [P, KC, QKV], F32R)
        wp = raw[:, n_end + KC * QKV:n_end + KC * QKV + KC * C].rearrange("p (k n) -> p k n", n=C)
        wph = sb("wph", [P, KC, C], F32R)
        wpl = sb("wpl", [P, KC, C], F32R)
        cs = sb("cs", [P, NT, 2, HD])

        sg = sb("sg", [P, 2, T])
        hf = sb("hf", [P, 2, T])
        hh = sb("hh", [P, HT, T], F32R)
        hl = sb("hl", [P, HT, T], F32R)
        delta = sb("delta", [P, 2, C])

        rot_a = sg[:, :, 0:ROT * HD].rearrange("p s (h d) -> p s h d", d=HD)
        rot_b = hf[:, 1, 0:ROT * HD].rearrange("p (h d) -> p h d", d=HD)
        rot = sb("rot", [P, 2, ROT, HD])
        qtok = sb("qtok", [P, NT, HEADS, ST], F32R)
        ktok = sb("ktok", [P, NT, KV, 2, ST], F32R)
        v_new, v_mid = (delta[:, half, :].rearrange("p (t g d) -> p t g d", t=NT, g=KV) for half in range(2))
        vtok = sb("vtok", [P, NT, KV, VW])
        qst = sb("qst", [P, HEADS // 2, T], F32R)
        kst = sb("kst", [P, KV, T], F32R)
        mneg = sb("mneg", [P, 2, NT, 4])
        mpad = [sb(f"mpart{i}", [P, NT * 8 + P - 8], F32R) for i in range(2)]
        mpart = [m[:, 0:NT * 8].rearrange("p (j half pair part) -> p j half pair part", j=NT, half=2, pair=2) for m in mpad]
        mT = hl[0:8, KC:KC + 2, :]
        rec = sb("rec", [P, 16])
        o_sb = hf[:, 0, :]
        low_parts = mneg[:, 0, 0, :]
        low_rows = mneg[:, 0, 1, 0:1]
        low_most = mneg[0:1, 0, 2, 0:1]
        low_flag = rec[0:1, 0:1].bitcast(I32)
        ytok = sb("ytok", [P, NT, C])
        v_first = ytok[:, 0, :].rearrange("p (t g d) -> p t g d", t=NT, g=KV)
        yh, yl = hh[:, 0:KC, :], hl[:, 0:KC, :]

        x0_in, x_in, gate_in, up_in, down_in, scales_in, c_in = (
            sem(n) for n in ("x0_in", "x_in", "gate_in", "up_in", "down_in", "scales_in", "c_in"))
        const = sem("const")
        const_b = sem("const_b")
        pads = sem("pads")
        wf_ready = sem("wf_ready")
        wT_ready, wTh_done, wTl_done = sem("wT_ready"), sem("wTh_done"), sem("wTl_done")
        w3h_done, w3l_done = sem("w3h_done"), sem("w3l_done")
        stats_done, mv_done, veps_done, rstd_done = (sem(n) for n in ("stats_done", "mv_done", "veps_done", "rstd_done"))
        xn_done, xT_ready, xh_done, xl_done = (sem(n) for n in ("xn_done", "xT_ready", "xh_done", "xl_done"))
        gate_ready, up_ready, silu_done = sem("gate_ready"), sem("up_ready"), sem("silu_done")
        h_done, hh_done, hl_done, down_done = (sem(n) for n in ("h_done", "hh_done", "hl_done", "down_done"))
        delta_done, x_done = sem("delta_done"), sem("x_done")
        qkv_ready, v_done, rot_ab, rot_done = (sem(n) for n in ("qkv_ready", "v_done", "rot_ab", "rot_done"))
        hi_done, lo_done = sem("hi_done"), sem("lo_done")
        stack_ready, stack_done = sem("stack_ready"), sem("stack_done")
        s_ready, smax_done = sem("s_ready"), sem("smax_done")
        mh_done, ml_done, mT_ready, mT_done = (sem(n) for n in ("mh_done", "ml_done", "mT_ready", "mT_done"))
        m_rows = [sem("m_rows0"), sem("m_rows1")]
        p_ready, exp_done, sel_done, pv_done = (sem(n) for n in ("p_ready", "exp_done", "sel_done", "pv_done"))
        o_done, oT_ready, rec_done, y_done = (sem(n) for n in ("o_done", "oT_ready", "rec_done", "y_done"))
        yT_ready, yh_done, yl_done, proj_ready = (sem(n) for n in ("yT_ready", "yh_done", "yl_done", "proj_ready"))
        stored = sem("stored")
        low_read, low_rows_done, low_row_ready, low_flag_done = (
            sem(n) for n in ("low_read", "low_rows_done", "low_row_ready", "low_flag_done"))
        v_moved, v_in = sem("v_moved"), sem("v_in")
        sum_done = sem("sum_done")
        dve_turn, pool_turn = sem("dve_turn"), sem("pool_turn")

        x_rows = x.rearrange("b (t p) c -> p (b t) c", p=P)
        out_rows = out.rearrange("b (t p) c -> p (b t) c", p=P)
        GU_PARTS = [(first, k) for first in range(0, 2 * FULL + 1, 4) for k in range(KC)]
        C_DMAS = 5
        PRIMED = 1
        primed = dict(pe=[down_done, mT_ready, pv_done], dve=[h_done, x_done, yl_done, y_done, ml_done, rot_done],
                      act=[hi_done, o_done, mT_done], pool=[hl_done, lo_done])
        PADS = 7

        def ring_bank(key):
            return bank[RING.index(key) % S_BANKS]

        def read_done(key):
            kind, a = key[0], key[1:]
            if kind == "s":
                return smax_done, KV * UNITS_S, UNITS_S * a[0] + a[1] + 1
            if kind == "stack":
                return stack_done, 3 * KV, 3 * a[0] + a[1] + 1
            if kind == "x":
                return xl_done, KC, KC * (B + 1) + a[0] + 1
            if kind == "qkv":
                return rot_ab, 3 * NT, 3 * (NT + a[0] + 1)
            if kind == "y":
                return yl_done, KC, PRIMED - KC + a[0] + 1
            return x_done, X_PER_CHUNK, PRIMED + X_PER_CHUNK * (B - 1) + a[0] + 1

        X_PER_CHUNK = 2

        def tiles(c, first, count):
            return bass.ds(c * NT + first, count)

        def pipeline(eng, iteration):
            iteration(0)
            with eng.Fori(1, B - 1) as b:
                iteration(b)
            iteration(B - 1)
            iteration(B)

        block = ctx.enter_context(nc.Block())

        @block.sync
        def _(sp):
            sp.dma_start(wi[:, 0:FULL, :], w_gate[0:FULL * P, :].rearrange("(m p) c -> p m c", p=P)).then_inc(gate_in, 16)
            sp.dma_start(X[:, 0:NT, :], x_rows[:, 0:NT, :]).then_inc(x0_in, 16)
            sp.dma_start(wi[REST:P, FULL, :], w_gate[FULL * P:HID, :]).then_inc(up_in, 16)
            sp.dma_start(wi[0:REST, FULL, :], w_up[FULL * P:HID, :]).then_inc(up_in, 16)
            sp.dma_start(wi[:, FULL + 1:, :], w_up[0:FULL * P, :].rearrange("(m p) c -> p m c", p=P)).then_inc(up_in, 16)
            sp.dma_start(wdi[:, :, :], w_down.rearrange("(m p) h -> p m h", p=P)).then_inc(down_in, 16)
            with nc.allow_non_contiguous_dma("scales, one per hidden row"):
                sp.dma_start(s_gu[:, 0:FULL], s_gate[0:FULL * P].rearrange("(m p) -> p m", p=P)).then_inc(scales_in, 16)
                sp.dma_start(s_gu[REST:P, FULL:FULL + 1], s_gate[FULL * P:HID].rearrange("(p a) -> p a", a=1)).then_inc(scales_in, 16)
                sp.dma_start(s_gu[0:REST, FULL:FULL + 1], s_up[FULL * P:HID].rearrange("(p a) -> p a", a=1)).then_inc(scales_in, 16)
                sp.dma_start(s_gu[:, FULL + 1:], s_up[0:FULL * P].rearrange("(m p) -> p m", p=P)).then_inc(scales_in, 16)
            sp.dma_start(sd_raw[:, :], s_down.rearrange("(a c) -> a c", a=1).to_broadcast([P, C])).then_inc(scales_in, 16)
            sp.dma_start(X[:, NT:, :], x_rows[:, NT:, :]).then_inc(x_in, 16)
            sp.dma_start(w3[:, :, 0:C], wq.rearrange("(k p) n -> p k n", p=P)).then_inc(c_in, 16)
            sp.dma_start(w3[:, :, C:QK], wk.rearrange("(k p) n -> p k n", p=P)).then_inc(c_in, 16)
            sp.dma_start(w3[:, :, QK:QKV], wv.rearrange("(k p) n -> p k n", p=P)).then_inc(c_in, 16)
            sp.dma_start(wp[:, :, :], wproj.rearrange("(k p) n -> p k n", p=P)).then_inc(c_in, 16)
            sp.dma_start(cs[:, :, :, :], rope).then_inc(c_in, 16)

            for s in m_rows:
                sp.sem_inc(s, 16 * PRIMED)

            def batch(b):
                for g in range(KV):
                    sp.wait_ge(mT_done, PRIMED + KV * b + g + 1)
                    for half in range(2):
                        for pair in range(2):
                            row = ST * half + 3 * HD
                            src = 4 * half + 2 * pair
                            sp.dma_start(qst[row:row + 2, 2 * g + pair, :].bitcast(F32),
                                         mT[src:src + 2, g % 2, :].bitcast(F32)).then_inc(m_rows[g % 2], 16)

            with sp.Fori(0, B) as b:
                batch(b)

            with sp.Fori(0, B) as c:
                sp.wait_ge(x_done, PRIMED + 2 * B * X_PER_CHUNK + X_PER_CHUNK * (c + 1))
                sp.dma_start(out_rows[:, tiles(c, 0, NT), :], X[:, tiles(c, 0, NT), :]).then_inc(stored, 16)
            sp.wait_ge(stored, 16 * B)

        @block.tensor
        def _(pe):
            def split3(acc, ah, al, bh, bl, start, stop, check=False):
                pe.matmul(acc, ah, bh, start=start, stop=False, skip_group_check=check)
                if bl is not None:
                    last = pe.matmul(acc, ah, bl, start=False, stop=(stop and al is None), skip_group_check=check)
                if al is not None:
                    last = pe.matmul(acc, al, bh, start=False, stop=stop, skip_group_check=check)
                return last

            def transpose_gate_up():
                for n, (first, k) in enumerate(GU_PARTS):
                    pe.wait_ge(wf_ready, 1 if first == 0 else 2)
                    if n >= 4:
                        pe.wait_ge(wTl_done, n - 3)
                    for m in range(min(4, 2 * FULL + 1 - first)):
                        last = pe.transpose(gu_bank[n % 4][:, P * m:P * m + P],
                                            wf[:, first + m, P * k:P * k + P], ident[:, :])
                    last.then_inc(wT_ready, 1)

            def transpose_down():
                pe.wait_ge(wf_ready, 3)
                for n, kt in enumerate(range(0, HT, 2)):
                    if n == 2:
                        pe.wait_ge(wTl_done, len(GU_PARTS) + 1)
                    for i in range(2):
                        for m in range(KC):
                            rows = P if kt + i < FULL else REST
                            last = pe.transpose(down_bank[n % 2][0:rows, C * i + P * m:C * i + P * m + P],
                                                wdf[:, m, P * (kt + i):P * (kt + i) + rows], ident[:, :])
                    last.then_inc(wT_ready, 1)

            def transpose_x(n, banks=tr_bank):
                pe.wait_ge(xn_done, NT * n + NT)
                pe.wait_ge(xl_done, KC * n)
                for k in range(KC):
                    for t in range(NT):
                        last = pe.transpose(banks[k][:, P * t:P * t + P], xn[:, t, P * k:P * k + P], ident[:, :])
                    last.then_inc(xT_ready, 1)

            def hidden(n, acc, m, low):
                for k in range(KC):
                    cols = slice(P * m, P * m + P)
                    last = split3(acc, guh[:, k, cols], gul[:, k, cols] if low else None, xh[:, k, :], xl[:, k, :],
                                  start=(k == 0), stop=(k == KC - 1))
                return last

            def gate_up(n, i, low):
                pe.wait_ge(h_done, PRIMED + HT * n + max(i - 1, 0))
                if i < FULL:
                    hidden(n, gu_bank[2 * i % 4][:, :], i, low).then_inc(gate_ready, 1)
                    hidden(n, gu_bank[(2 * i + 1) % 4][:, :], FULL + 1 + i, low).then_inc(up_ready, 1)
                else:
                    hidden(n, gu_bank[2 * i % 4][:, :], FULL, low).then_inc(gate_ready, 1)

            def down(n, kt, low):
                pe.wait_ge(hl_done, PRIMED + HT * n + kt + 1)
                rows = P if kt < FULL else REST
                for t in range(NT):
                    cols = slice(P * t, P * t + P)
                    last = split3(down_bank[t // 2][:, C * (t % 2):C * (t % 2) + C],
                                  hh[0:rows, kt, cols], hl[0:rows, kt, cols], dh[0:rows, kt, :],
                                  dl[0:rows, kt, :] if low else None,
                                  start=(kt == 0 and t % 2 == 0), stop=(kt == HT - 1), check=True)
                last.then_inc(down_done, 1)

            def chunk(stage, c, following, low, first=False):
                n = c + (B if stage else 0)
                pe.wait_ge(xl_done, KC * (c + stage * B) + KC)
                gate_up(n, 0, low)
                gate_up(n, 1, low)
                gate_up(n, 2, low)
                pe.wait_ge(x_done, PRIMED + X_PER_CHUNK * (c + stage * B))
                if first:
                    pe.wait_ge(wTl_done, len(GU_PARTS) + 3)
                down(n, 0, low)
                gate_up(n, 3, low)
                down(n, 1, low)
                gate_up(n, 4, low)
                down(n, 2, low)
                gate_up(n, 5, low)
                if first:
                    pe.wait_ge(low_rows_done, 1)
                    pe.transpose(gu_bank[3][0:1, 0:P], low_rows[:, :], ident[:, :]).then_inc(low_row_ready, 1)
                down(n, 3, low)
                if following is not None:
                    transpose_x(c + stage * B + 1)
                for kt in range(4, HT):
                    down(n, kt, low)

            def chunks(stage, low):
                with pe.Fori(0 if stage else 1, B - 1) as c:
                    chunk(stage, c, c + 1, low)
                chunk(stage, B - 1, None if stage else 0, low)

            def ffn(stage, any_low):
                with pe.If(any_low):
                    chunks(stage, True)
                with pe.Else():
                    chunks(stage, False)

            def attention():
                def take_bank(key, b):
                    at = RING.index(key)
                    for i in range(at - S_BANKS, -1, -S_BANKS):
                        if present(RING[i], b):
                            done, per, offset = read_done(RING[i])
                            pe.wait_ge(done, per * b + offset)
                            return
                    if isinstance(b, int) and b < 0:
                        return
                    if at == 0 and live(b, 0) and live(b, -1):
                        pe.wait_ge(smax_done, KV * UNITS_S * b - 2)
                    for i in range(len(RING) - 1, -1, -1):
                        if i % S_BANKS == at % S_BANKS and present(RING[i], b - 1 if isinstance(b, int) else b):
                            done, per, offset = read_done(RING[i])
                            pe.wait_ge(done, per * b + offset - per)
                            return

                def qkv(b, t):
                    if t == 0:
                        pe.wait_ge(xl_done, KC * b + KC * (B + 2))
                    cols = slice(P * t, P * t + P)
                    for k in range(KC):
                        last = split3(ring_bank(("qkv", t))[:, 0:QKV], xh[:, k, cols], xl[:, k, cols],
                                      w3h[:, k, :], w3l[:, k, :], start=(k == 0), stop=(k == KC - 1))
                    last.then_inc(qkv_ready, 1)

                def stack(b, g, j):
                    if g == KV:
                        pe.wait_ge(lo_done, PRIMED + 2 * NT * 2 + 2 * NT * b)
                    for t in range(NT):
                        if j == 0:
                            src = ktok[:, t, g % KV, :, :].rearrange("p a s -> p (a s)")
                        else:
                            first = 4 * (g % KV) + 2 * (j - 1)
                            src = qtok[:, t, first:first + 2, :].rearrange("p a s -> p (a s)")
                        last = pe.transpose(ring_bank(("stack", g, j))[:, P * t:P * t + P], src.bitcast(F32), ident[:, :])
                    last.then_inc(stack_ready, 1)

                def transposes(src, acc, k, ready):
                    for t in range(NT):
                        last = pe.transpose(acc[:, P * t:P * t + P], src[:, t, P * k:P * k + P], ident[:, :])
                    last.then_inc(ready, 1)

                def project(b, p):
                    if p == 0:
                        pe.wait_ge(yl_done, PRIMED + KC * b)
                    acc = ring_bank(("proj", p))
                    for t in (2 * p, 2 * p + 1):
                        cols = slice(P * t, P * t + P)
                        for k in range(KC):
                            last = split3(acc[:, C * (t % 2):C * (t % 2) + C], yh[:, k, cols], yl[:, k, cols],
                                          wph[:, k, :], wpl[:, k, :], start=(k == 0), stop=(k == KC - 1))
                    last.then_inc(proj_ready, 1)

                def job(b, key):
                    take_bank(key, b)
                    if key[0] == "stack":
                        stack(b, key[1], key[2])
                    elif key[0] == "x":
                        if key[1] == 0:
                            pe.wait_ge(xn_done, NT * b + NT * (B + 2))
                        transposes(xn, ring_bank(key), key[1], xT_ready)
                    elif key[0] == "qkv":
                        qkv(b, key[1])
                    elif key[0] == "y":
                        if key[1] == 0:
                            pe.wait_ge(y_done, PRIMED + KV * b)
                        transposes(ytok, ring_bank(key), key[1], yT_ready)
                    else:
                        project(b, key[1])

                def scores(b, g, i):
                    if i == 0:
                        pe.wait_ge(stack_done, 3 * KV * b + 3 * (g + 1))
                    take_bank(("s", g, i), b)
                    acc = ring_bank(("s", g, i))
                    j, heads = score_units()[i]
                    keys = P * (j + 1)
                    n = len(heads)
                    for a, h in enumerate(heads):
                        rows = slice(ST * (h % 2), ST * (h % 2) + ST)
                        pe.matmul(acc[:, keys * a:keys * a + keys],
                                  qst[rows, 2 * g + h // 2, P * j:P * j + P], kst[rows, g, 0:keys],
                                  start=(a == 0), stop=False, skip_group_check=True)
                    diagonal = acc[:, 0:keys * n].rearrange("p (a k) -> p a k", k=keys)[:, :, keys - P:keys]
                    pe.matmul(diagonal, ident_b[:, :], causal_b[:, 0:n, :], start=False, stop=True,
                              skip_group_check=True).then_inc(s_ready, 1)

                def maxima(b, g):
                    pe.wait_ge(ml_done, PRIMED + KV * b + g + 1)
                    if live(b, g - 4):
                        pe.wait_ge(y_done, PRIMED + KV * b + g - 3)
                    elif live(b, g - 1):
                        pe.wait_ge(mT_done, PRIMED + KV * b + g)
                    else:
                        pe.wait_ge(x_done, PRIMED + X_PER_CHUNK * B)
                    for j in range(NT):
                        last = pe.transpose(m_bank[:, P * j:P * j + P], mpad[g % 2][:, 8 * j:8 * j + P].bitcast(F32), ident[:, :])
                    last.then_inc(mT_ready, 1)

                def shifted(b, g, i):
                    w = UNITS_P * (g + 2) + i
                    if i == 0:
                        pe.wait_ge(m_rows[g % 2], 16 * 4 * 2 * b + 16 * (PRIMED + 4 * (g // 2 + 1)))
                    if live(b, g - 1) or i >= P_BANKS:
                        pe.wait_ge(exp_done, KV * UNITS_P * b + UNITS_P * g + i - P_BANKS + 1)
                    blocks = prob_units()[i]
                    for a, (h, kt, col) in enumerate(blocks):
                        rows = slice(ST * (h % 2), ST * (h % 2) + ST)
                        n = T - P * kt
                        last = pe.matmul(p_bank[w % P_BANKS][:, col:col + n],
                                         kst[rows, g % KV, P * kt:P * kt + P], qst[rows, 2 * (g % KV) + h // 2, P * kt:T],
                                         start=(a == 0), stop=(a == len(blocks) - 1), skip_group_check=True)
                    last.then_inc(p_ready, 1)

                def values(b, g, kt):
                    if kt == 0:
                        pe.wait_ge(o_done, PRIMED + KV * b + g)
                        pe.wait_ge(v_in, KV * b + g + 1)
                    pe.wait_ge(sel_done, 4 * KV * b + 4 * g + (1, 2, 4, 3)[kt])
                    for h in range(4):
                        u, col = prob_place(h, kt, kt)
                        last = pe.matmul(pv_bank[VW * h:VW * h + VW, P * kt:T], vtok[:, kt, g % KV, :],
                                         pT[:, g % 2, u, col:col + T - P * kt], start=(kt == 0), stop=(kt == NT - 1))
                    if kt == NT - 1:
                        last.then_inc(pv_done, 1)

                def outputs(b, g):
                    pe.wait_ge(o_done, PRIMED + KV * b + g + 1)
                    if live(b, g + 3):
                        pe.wait_ge(mT_done, PRIMED + KV * b + g + 4)
                    else:
                        pe.wait_ge(y_done, PRIMED + KV * b + g)
                    for j in range(NT):
                        last = pe.transpose(m_bank[:, P * j:P * j + P], o_sb[:, P * j:P * j + P], ident[:, :])
                    last.then_inc(oT_ready, 1)

                def iteration(b):
                    for slot, i in STEPS:
                        key = JOBS.get((slot, i))
                        if key and present(key, b):
                            job(b, key)
                        if live(b, slot) and present(("s",), b):
                            scores(b, slot, i)
                        if i == 2 and live(b, slot - 1):
                            maxima(b, slot - 1)
                        if i == OUTPUTS_AT and live(b, slot - 4):
                            outputs(b, slot - 4)
                        if i < UNITS_P and live(b, slot - 2):
                            shifted(b, slot - 2, i)
                        if i in VALUES_AT and live(b, slot - 3):
                            values(b, slot - 3, VALUES_AT.index(i))

                pe.wait_ge(h_done, PRIMED + HT * B)
                pe.wait_ge(const_b, 3)
                pe.wait_ge(w3l_done, 2)
                pe.wait_ge(pads, PADS)
                iteration(-1)
                pipeline(pe, iteration)

            for s in primed["pe"]:
                pe.sem_inc(s, PRIMED)
            pe.wait_ge(const, 2)
            transpose_gate_up()
            transpose_x(0)
            transpose_down()
            pe.wait_ge(wTl_done, len(GU_PARTS))
            chunk(0, 0, 1, True, first=True)
            pe.wait_ge(low_flag_done, 1)
            any_low = pe.value_load(low_flag[0:1, 0:1], min_val=0, max_val=1)
            ffn(0, any_low)
            attention()
            pe.wait_ge(x_done, PRIMED + 2 * X_PER_CHUNK * B)
            ffn(2, any_low)

        @block.vector
        def _(dve):
            def row_stats(n, c):
                for t in range(NT):
                    dve.bn_stats(stats[:, t, :], X[:, tiles(c, t, 1), :].rearrange("p a c -> p (a c)")).then_inc(stats_done, 1)
                dve.wait_ge(rstd_done, n)
                dve.wait_ge(stats_done, NT * n + NT)
                dve.sem_inc(dve_turn, 1)
                for t in range(NT):
                    dve.bn_aggr(mv[:, t, :], stats[:, t, :]).then_inc(mv_done, 1)

            def row_sums(n, c):
                dve.wait_ge(sum_done, 2 * n)
                dve.sem_inc(dve_turn, 1)
                dve.tensor_reduce(part_sum[:, :, :], X[:, tiles(c, 0, NT), :].rearrange("p t (a k) -> p t a k", k=16),
                                  AX.X, ALU.add).then_inc(sum_done, 1)
                dve.wait_ge(sum_done, 2 * n + 1)
                dve.tensor_reduce(row_sum[:, :], part_sum[:, :, :], AX.X, ALU.add).then_inc(sum_done, 1)

            def normalize(n, c):
                dve.wait_ge(rstd_done, n + 1)
                dve.wait_ge(xT_ready, KC * n)
                for t in range(NT):
                    dve.tensor_scalar(xn[:, t, :], X[:, tiles(c, t, 1), :].rearrange("p a c -> p (a c)"),
                                      mean[:, t:t + 1], rstd[:, t:t + 1], ALU.subtract, ALU.mult).then_inc(xn_done, 1)

            def low_x(n, banks=tr_bank):
                for k in range(KC):
                    dve.wait_ge(xh_done, KC * n + k + 1)
                    dve.tensor_tensor(xl[:, k, :], banks[k][:, :], xh[:, k, :].bitcast(F32), ALU.subtract).then_inc(xl_done, 1)

            def prepare():
                dve.wait_ge(gate_in, 16)
                dve.tensor_scalar(wf[:, 0:FULL, :], wi[:, 0:FULL, :], 128.0, None, ALU.subtract).then_inc(wf_ready, 1)
                dve.wait_ge(x0_in, 16)
                row_stats(0, 0)
                row_sums(0, 0)
                dve.wait_ge(up_in, 3 * 16)
                dve.tensor_scalar(wf[:, FULL:, :], wi[:, FULL:, :], 128.0, None, ALU.subtract).then_inc(wf_ready, 1)
                for n, (first, k) in enumerate(GU_PARTS):
                    a, b = P * first, min(P * (first + 4), 2 * HID)
                    dve.wait_ge(wTh_done, n + 1)
                    dve.tensor_tensor(gul[:, k, a:b], gu_bank[n % 4][:, 0:b - a], guh[:, k, a:b].bitcast(F32),
                                      ALU.subtract).then_inc(wTl_done, 1)
                    if n == 1:
                        normalize(0, 0)
                    if n == 2:
                        dve.wait_ge(down_in, 16)
                        dve.tensor_scalar(wdf[:, :, :], wdi[:, :, :], 128.0, None, ALU.subtract).then_inc(wf_ready, 1)
                low_x(0)
                for n, kt in enumerate(range(0, HT, 2)):
                    dve.wait_ge(wTh_done, len(GU_PARTS) + n + 1)
                    acc = down_bank[n % 2]
                    if kt + 1 < FULL:
                        dve.tensor_tensor(dl[:, kt:kt + 2, :].rearrange("p a c -> p (a c)"), acc[:, :],
                                          dh[:, kt:kt + 2, :].rearrange("p a c -> p (a c)").bitcast(F32),
                                          ALU.subtract).then_inc(wTl_done, 1)
                    else:
                        dve.tensor_tensor(dl[:, kt, :], acc[:, 0:C], dh[:, kt, :].bitcast(F32), ALU.subtract)
                        dve.tensor_tensor(dl[0:REST, kt + 1, :], acc[0:REST, C:2 * C],
                                          dh[0:REST, kt + 1, :].bitcast(F32), ALU.subtract).then_inc(wTl_done, 1)
                dve.wait_ge(scales_in, 5 * 16)
                dve.tensor_scalar(sd_half[:, :], sd_raw[:, :], 0.5, None, ALU.mult).then_inc(wf_ready, 1)

            def add_down(stage, c, p):
                n = c + (B if stage else 0)
                done = PRIMED + X_PER_CHUNK * stage * B + p
                if p == 0:
                    dve.wait_ge(down_done, PRIMED + HT * n + HT)
                dve.wait_ge(x_done, X_PER_CHUNK * c + done)
                dve.tensor_tensor(delta[:, :, :], down_bank[p][:, :].rearrange("p (a c) -> p a c", a=2),
                                  sd_half[:, :].rearrange("p (a c) -> p a c", a=1).to_broadcast([P, 2, C]),
                                  ALU.mult).then_inc(delta_done, 1)
                dve.wait_ge(delta_done, 2 * n + p + 1)
                rows = X[:, tiles(c, 2 * p, 2), :]
                dve.tensor_tensor(rows, rows, delta[:, :, :], ALU.add).then_inc(x_done, 1)

            def ffn(base, stage):
                def hidden(n, i):
                    rows = P if i < FULL else REST
                    dve.wait_ge(silu_done, HT * n + i + 1)
                    if i < FULL:
                        dve.wait_ge(up_ready, FULL * n + i + 1)
                    dve.wait_ge(hl_done, PRIMED + HT * n + max(i - 1, 0))
                    u, s = ((2 * i + 1) % 4, FULL + 1 + i) if i < FULL else (2 * i % 4, FULL)
                    dve.scalar_tensor_tensor(hf[0:rows, i % 2, :], gu_bank[u][0:rows, :], s_gu[0:rows, s:s + 1],
                                             sg[0:rows, i % 2, :], ALU.mult, ALU.mult).then_inc(h_done, 1)

                def largest_low(i, low, rows=P):
                    dve.tensor_reduce(low_parts[0:rows, i:i + 1], low, AX.X, ALU.max, apply_absolute_value=True).then_inc(low_read, 1)

                def chunk(c, following, first=False):
                    n = c + base
                    nx = c + stage * B + 1
                    before = not isinstance(c, int) or c > 0
                    if before:
                        add_down(stage, c - 1, 0)
                    hidden(n, 0)
                    if before:
                        add_down(stage, c - 1, 1)
                    hidden(n, 1)
                    if first:
                        largest_low(0, gul[:, 0, :].bitcast(F32))
                    if following is not None:
                        row_stats(nx, following)
                    if following is not None:
                        row_sums(nx, following)
                    hidden(n, 2)
                    if first:
                        largest_low(1, gul[:, 1, :].bitcast(F32))
                    hidden(n, 3)
                    if following is not None:
                        normalize(nx, following)
                    if first:
                        largest_low(2, dl[:, 0:FULL, :].rearrange("p m c -> p (m c)").bitcast(F32))
                        largest_low(3, dl[0:REST, FULL, :].bitcast(F32), REST)
                        dve.wait_ge(low_read, 4)
                        dve.tensor_reduce(low_rows[:, :], low_parts[:, :], AX.X, ALU.max).then_inc(low_rows_done, 1)
                    hidden(n, 4)
                    hidden(n, 5)
                    if first:
                        dve.wait_ge(low_row_ready, 1)
                        dve.tensor_reduce(low_most[:, :], gu_bank[3][0:1, 0:P], AX.X, ALU.max).then_inc(low_read, 1)
                        dve.wait_ge(low_read, 5)
                        dve.tensor_scalar(low_flag[:, :], low_most[:, :], 0.0, None, ALU.is_gt).then_inc(low_flag_done, 1)
                    if following is not None:
                        low_x(nx)

                chunk(0, 1, first=(stage == 0))
                with dve.Fori(1, B - 1) as c:
                    chunk(c, c + 1)
                chunk(B - 1, 0 if stage == 0 else None)
                if stage:
                    for p in range(2):
                        add_down(stage, B - 1, p)

            def attention():
                def rotary(b, t):
                    s = t % 2
                    n = NT * b + NT + t
                    qk = ring_bank(("qkv", t))[:, 0:QK].rearrange("p (h d) -> p h d", d=HD)
                    dve.wait_ge(v_done, n + 1)
                    dve.wait_ge(rot_done, n + PRIMED)

                    def table(which, a, z):
                        return cs[:, t, which, a:z].rearrange("p (a d) -> p a d", a=1).to_broadcast([P, ROT, z - a])
                    half = HD // 2
                    dve.tensor_tensor(rot_a[:, s, :, :], qk, table(0, 0, HD), ALU.mult).then_inc(rot_ab, 1)
                    dve.tensor_tensor(rot_b[:, :, 0:half], qk[:, :, half:HD], table(1, 0, half), ALU.mult).then_inc(rot_ab, 1)
                    dve.tensor_tensor(rot_b[:, :, half:HD], qk[:, :, 0:half], table(1, half, HD), ALU.mult).then_inc(rot_ab, 1)
                    dve.wait_ge(rot_ab, 3 * n + 3)
                    before = NT * b + NT + max(t - 1, 0)
                    dve.wait_ge(hi_done, 6 * before + PRIMED)
                    dve.wait_ge(lo_done, 2 * before + PRIMED)
                    dve.tensor_tensor(rot[:, s, :, :], rot_a[:, s, :, :], rot_b[:, :, :], ALU.add).then_inc(rot_done, 1)

                def row_max(b, g, i):
                    j, heads = score_units()[i]
                    keys = P * (j + 1)
                    if i == 0 and live(b, g - 1):
                        dve.wait_ge(ml_done, PRIMED + KV * b + g)
                    dve.wait_ge(s_ready, KV * UNITS_S * b + UNITS_S * g + i + 1)
                    dst = mneg[:, g % 2, j, heads[0]:heads[-1] + 1:2] if len(heads) == 2 else \
                        mneg[:, g % 2, j, heads[0]:heads[0] + 1]
                    acc = ring_bank(("s", g, i))
                    dve.tensor_reduce(dst, acc[:, 0:keys * len(heads)].rearrange("p (a k) -> p a k", k=keys),
                                      AX.X, ALU.max, negate=True).then_inc(smax_done, 1)

                def split_max(b, g):
                    dve.wait_ge(smax_done, KV * UNITS_S * b + UNITS_S * (g + 1))
                    if live(b, g - 1):
                        dve.wait_ge(mT_ready, PRIMED + KV * b + g - 1 + (g == 0))
                    src = mneg[:, g % 2, :, :].rearrange("p j (pair half) -> p j half pair", half=2)
                    for half in range(2):
                        dve.tensor_copy(mpart[g % 2][:, :, half, :, 0], src[:, :, half, :]).then_inc(mh_done, 1)
                    for half in range(2):
                        dve.wait_ge(mh_done, 2 * KV * b + 2 * g + 1 + half)
                        last = dve.tensor_tensor(mpart[g % 2][:, :, half, :, 1], src[:, :, half, :],
                                                 mpart[g % 2][:, :, half, :, 0].bitcast(F32), ALU.subtract)
                    last.then_inc(ml_done, 1)

                def heads_out(b, g):
                    dve.wait_ge(oT_ready, KV * b + g - KV + 1)
                    dve.wait_ge(y_done, PRIMED + KV * b + g - KV)
                    o = m_bank[:, :].rearrange("p (j h d) -> p j h d", j=NT, h=4)
                    dve.reciprocal(rec[:, :], m_bank[:, HD:512:VW]).then_inc(rec_done, 1)
                    dve.wait_ge(rec_done, KV * b + g - KV + 1)
                    inv = rec[:, :].rearrange("p (j h a) -> p j h a", j=NT, a=1).to_broadcast([P, NT, 4, HD])
                    dst = ytok[:, :, 64 * g:64 * g + 64].rearrange("p j (h d) -> p j h d", h=4)
                    dve.tensor_tensor(dst, o[:, :, :, 0:HD], inv, ALU.mult).then_inc(y_done, 1)

                def read_job(b, key):
                    kind, at = key[0], key[1]
                    if kind == "x":
                        dve.wait_ge(xh_done, KC * b + KC * (B + 1) + at + 1)
                        dve.tensor_tensor(xl[:, at, :], ring_bank(key)[:, :], xh[:, at, :].bitcast(F32),
                                          ALU.subtract).then_inc(xl_done, 1)
                    elif kind == "qkv":
                        rotary(b, at)
                    elif kind == "y":
                        dve.wait_ge(yh_done, KC * b - KC + at + 1)
                        dve.tensor_tensor(yl[:, at, :], ring_bank(key)[:, :], yh[:, at, :].bitcast(F32),
                                          ALU.subtract).then_inc(yl_done, 1)
                    elif kind == "proj":
                        dve.wait_ge(proj_ready, 2 * b - 2 + at + 1)
                        rows = X[:, tiles(b, 2 * at - NT, 2), :]
                        dve.tensor_tensor(rows, ring_bank(key)[:, :].rearrange("p (a c) -> p a c", a=2), rows,
                                          ALU.add).then_inc(x_done, 1)

                def iteration(b):
                    following = 0 if isinstance(b, int) and b == B - 1 else b + 1
                    for slot, i in STEPS:
                        if present(("s",), b):
                            row_max(b, slot, i)
                        key = JOBS.get((slot, i))
                        if key and present(key, b):
                            read_job(b, key)
                        if i == UNITS_S - 1 and present(("s",), b):
                            split_max(b, slot)
                        if i == HEADS_AT and live(b, slot - 4):
                            heads_out(b, slot)
                        if present(("x",), b):
                            if (slot, i) == STATS_AT:
                                row_stats(b + B + 1, following)
                            if (slot, i) == SUMS_AT:
                                row_sums(b + B + 1, following)
                            if (slot, i) == NORMALIZE_AT:
                                normalize(b + B + 1, following)

                dve.wait_ge(c_in, 16 * C_DMAS)
                for t in range(NT):
                    rotary(-1, t)
                for p in range(2):
                    add_down(0, B - 1, p)
                pipeline(dve, iteration)

            for s in primed["dve"]:
                dve.sem_inc(s, PRIMED)
            prepare()
            dve.wait_ge(const, 6)
            dve.wait_ge(x_in, 16)
            dve.wait_ge(wf_ready, 4)
            ffn(0, 0)
            attention()
            ffn(B, 2)

        @block.scalar
        def _(act):
            def high_x(n, banks=tr_bank):
                for k in range(KC):
                    act.wait_ge(xT_ready, KC * n + k + 1)
                    act.activation(xh[:, k, :], banks[k][:, :], ACT.Copy).then_inc(xh_done, 1)

            def prepare():
                for n, (first, k) in enumerate(GU_PARTS):
                    a, b = P * first, min(P * (first + 4), 2 * HID)
                    act.wait_ge(wT_ready, n + 1)
                    act.activation(guh[:, k, a:b], gu_bank[n % 4][:, 0:b - a], ACT.Copy).then_inc(wTh_done, 1)
                high_x(0)
                for n, kt in enumerate(range(0, HT, 2)):
                    act.wait_ge(wT_ready, len(GU_PARTS) + n + 1)
                    acc = down_bank[n % 2]
                    if kt + 1 < FULL:
                        act.activation(dh[:, kt:kt + 2, :].rearrange("p a c -> p (a c)"), acc[:, :],
                                       ACT.Copy).then_inc(wTh_done, 1)
                    else:
                        act.activation(dh[:, kt, :], acc[:, 0:C], ACT.Copy).then_inc(w3h_done, 1)
                        act.activation(dh[0:REST, kt + 1, :], acc[0:REST, C:2 * C], ACT.Copy).then_inc(w3h_done, 1)
                        act.wait_ge(w3h_done, 2)
                        act.sem_inc(wTh_done, 1)

            def split_projections():
                act.wait_ge(c_in, 16 * C_DMAS)
                act.activation(w3h[:, :, :], w3[:, :, :], ACT.Copy).then_inc(w3h_done, 1)
                act.activation(wph[:, :, :], wp[:, :, :], ACT.Copy).then_inc(w3h_done, 1)

            def ffn(base, stage):
                def silu(n, i):
                    rows = slice(0, P) if i < FULL else slice(REST, P)
                    m = i if i < FULL else FULL
                    act.wait_ge(gate_ready, HT * n + i + 1)
                    act.wait_ge(h_done, PRIMED + HT * n + max(i - 1, 0))
                    act.activation(sg[0:P - rows.start, i % 2, :], gu_bank[2 * i % 4][rows, :], ACT.Silu,
                                   scale=s_gu[rows, m:m + 1]).then_inc(silu_done, 1)

                def high_h(n, i):
                    rows = P if i < FULL else REST
                    act.wait_ge(h_done, PRIMED + HT * n + i + 1)
                    if i == 0:
                        act.wait_ge(down_done, PRIMED + HT * n)
                    act.activation(hh[0:rows, i, :], hf[0:rows, i % 2, :], ACT.Copy).then_inc(hh_done, 1)

                def chunk(c, following, first=False):
                    n = c + base
                    silu(n, 0)
                    for i in range(1, HT):
                        silu(n, i)
                        high_h(n, i - 1)
                        if first and i == 3:
                            split_projections()
                    high_h(n, HT - 1)
                    if following is not None:
                        high_x(c + stage * B + 1)

                if stage == 0:
                    chunk(0, 1, first=True)
                    with act.Fori(1, B - 1) as c:
                        chunk(c, c + 1)
                    chunk(B - 1, 0)
                else:
                    with act.Fori(0, B - 1) as c:
                        chunk(c, c + 1)
                    chunk(B - 1, None)

            def attention():
                def copy_outputs(b, g):
                    act.wait_ge(pv_done, PRIMED + KV * b + g + 1)
                    if live(b, g - 1):
                        act.wait_ge(oT_ready, KV * b + g)
                    act.activation(o_sb[:, :], pv_bank[:, :], ACT.Copy).then_inc(o_done, 1)

                def copy_values(b, t):
                    act.wait_ge(qkv_ready, NT * b + NT + t + 1)
                    if t == 0 and live(b, 0):
                        act.wait_ge(v_moved, b + 1)
                    staged = v_new if live(b, 0) else v_first
                    act.activation(staged[:, t, :, :], ring_bank(("qkv", t))[:, QK:QKV].rearrange("p (g d) -> p g d", d=HD),
                                   ACT.Copy).then_inc(v_done, 1)

                def high_qk(b, t):
                    s = t % 2
                    act.wait_ge(rot_done, PRIMED + NT + NT * b + t + 1)
                    for a in (0, 2):
                        act.activation(qtok[:, t, :, HD * a:HD * a + HD], rot[:, s, 0:HEADS, :], ACT.Copy).then_inc(hi_done, 1)
                    for half in range(2):
                        for a in range(2):
                            act.activation(ktok[:, t, :, half, HD * a:HD * a + HD], rot[:, s, HEADS:, :],
                                           ACT.Copy).then_inc(hi_done, 1)

                def copy_max(b, g):
                    act.wait_ge(mT_ready, PRIMED + KV * b + g + 1)
                    if live(b, g - 2):
                        act.wait_ge(m_rows[g % 2], 16 * 4 * 2 * b + 16 * (PRIMED + 4 * (g // 2)))
                    act.activation(mT[:, g % 2, :], m_bank[0:8, :], ACT.Copy).then_inc(mT_done, 1)

                def exps(b, g, i):
                    w = UNITS_P * (g + 2) + i
                    act.wait_ge(p_ready, KV * UNITS_P * b + UNITS_P * g + i + 1)
                    if i == 0 and live(b, g - 2):
                        act.wait_ge(pv_done, PRIMED + KV * b + g - 1)
                    act.activation(pT[:, g % 2, i, :], p_bank[w % P_BANKS][:, :], ACT.Exp,
                                   scale=float(HD) ** -0.5).then_inc(exp_done, 1)

                def read_job(b, key):
                    kind, at = key[0], key[1]
                    if kind == "stack":
                        g, j = key[1:]
                        act.wait_ge(stack_ready, 3 * KV * b + 3 * g + j + 1)
                        dst = kst[:, g % KV, :] if j == 0 else qst[:, 2 * (g % KV) + j - 1, :]
                        act.activation(dst, ring_bank(key)[:, :], ACT.Copy).then_inc(stack_done, 1)
                    elif kind == "x":
                        act.wait_ge(xT_ready, KC * b + KC * (B + 1) + at + 1)
                        act.activation(xh[:, at, :], ring_bank(key)[:, :], ACT.Copy).then_inc(xh_done, 1)
                    elif kind == "qkv":
                        copy_values(b, at)
                    elif kind == "y":
                        act.wait_ge(yT_ready, KC * b - KC + at + 1)
                        act.activation(yh[:, at, :], ring_bank(key)[:, :], ACT.Copy).then_inc(yh_done, 1)

                def iteration(b):
                    for slot, i in STEPS:
                        if i == 0 and live(b, slot - 4):
                            copy_outputs(b, slot - 4)
                        key = JOBS.get((slot, i))
                        if key and present(key, b):
                            read_job(b, key)
                        if (slot, i) in HIGH_AT and present(("qkv",), b):
                            high_qk(b, HIGH_AT.index((slot, i)))
                        if i < UNITS_P and live(b, slot - 2):
                            exps(b, slot - 2, i)
                        if i == 2 and live(b, slot - 1):
                            copy_max(b, slot - 1)

                copy_values(-1, 0)
                for t in range(NT):
                    if t + 1 < NT:
                        copy_values(-1, t + 1)
                    high_qk(-1, t)
                for step, key in JOBS.items():
                    if key[0] == "stack" and present(key, -1):
                        read_job(-1, key)
                pipeline(act, iteration)

            for s in primed["act"]:
                act.sem_inc(s, PRIMED)
            prepare()
            act.wait_ge(scales_in, 5 * 16)
            ffn(0, 0)
            attention()
            ffn(B, 2)

        @block.gpsimd
        def _(pool):
            def constants():
                pool.memset(ident[:, :], 1.0).then_inc(const, 1)
                pool.wait_ge(const, 1)
                pool.affine_select(out=ident[:, :], in_=ident[:, :], compare_op=ALU.is_equal, fill=0.0, base=0,
                                   pattern=[[1, P]], channel_multiplier=-1).then_inc(const, 1)
                pool.memset(low_parts[:, :], 0.0).then_inc(const, 1)
                pool.memset(neg_half[:, :], -0.5).then_inc(const, 1)
                pool.memset(inv_c[:, :], 1.0 / C).then_inc(const, 1)
                pool.memset(eps[:, :], EPS).then_inc(const, 1)
                pool.memset(causal_b[:, :, :], 0.0).then_inc(const_b, 1)
                pool.wait_ge(const, 2)
                pool.tensor_copy(ident_b[:, :], ident[:, :]).then_inc(const_b, 1)
                pool.wait_ge(const_b, 1)
                pool.affine_select(out=causal_b[:, :, :], in_=causal_b[:, :, :], compare_op=ALU.is_ge, fill=NEG, base=0,
                                   pattern=[[0, 2], [-1, P]], channel_multiplier=1).then_inc(const_b, 1)

            def padding():
                pool.memset(qtok[:, :, :, 3 * HD:].bitcast(F32), 0.0).then_inc(pads, 1)
                pool.memset(ktok[:, :, :, :, 3 * HD + 2:].bitcast(F32), 0.0).then_inc(pads, 1)
                pool.memset(ktok[:, :, :, :, 3 * HD:3 * HD + 2].bitcast(F32), 1.0).then_inc(pads, 1)
                pool.memset(vtok[:, :, :, HD:HD + 1], 1.0).then_inc(pads, 1)
                pool.memset(vtok[:, :, :, HD + 1:], 0.0).then_inc(pads, 1)
                for m in mpad:
                    pool.memset(m[:, :].bitcast(F32), 0.0).then_inc(pads, 1)

            def deviation(n):
                pool.wait_ge(mv_done, NT * n + NT)
                pool.wait_ge(xn_done, NT * n)
                pool.wait_ge(sum_done, 2 * n + 2)
                pool.tensor_tensor(mean[:, :], row_sum[:, :], inv_c[:, :], ALU.mult).then_inc(veps_done, 1)
                pool.tensor_tensor(veps[:, :], mv[:, :, 1], eps[:, :], ALU.add).then_inc(veps_done, 1)
                pool.wait_ge(veps_done, 2 * n + 2)
                pool.tensor_tensor(rstd[:, :], veps[:, :], neg_half[:, :], ALU.pow).then_inc(rstd_done, 1)

            def split_projections():
                pool.wait_ge(w3h_done, 3)
                pool.tensor_tensor(w3l[:, :, :], w3[:, :, :], w3h[:, :, :].bitcast(F32), ALU.subtract).then_inc(w3l_done, 1)
                pool.wait_ge(w3h_done, 4)
                pool.tensor_tensor(wpl[:, :, :], wp[:, :, :], wph[:, :, :].bitcast(F32), ALU.subtract).then_inc(w3l_done, 1)

            def ffn(base, stage):
                def low_h(n, i):
                    rows = P if i < FULL else REST
                    pool.wait_ge(hh_done, HT * n + i + 1)
                    pool.tensor_tensor(hl[0:rows, i, :], hf[0:rows, i % 2, :], hh[0:rows, i, :].bitcast(F32),
                                       ALU.subtract).then_inc(hl_done, 1)

                def chunk(c, following, first=False):
                    for i in range(HT):
                        low_h(c + base, i)
                        if first and i == 3:
                            split_projections()
                        if i == 1 and following is not None:
                            deviation(c + stage * B + 1)

                if stage == 0:
                    chunk(0, 1, first=True)
                    with pool.Fori(1, B - 1) as c:
                        chunk(c, c + 1)
                    chunk(B - 1, 0)
                else:
                    with pool.Fori(0, B - 1) as c:
                        chunk(c, c + 1)
                    chunk(B - 1, None)

            def attention():
                def wait_exp(count):
                    pool.wait_ge(exp_done, count)
                    pool.sem_inc(pool_turn, 1)

                def mask(g, first, count, col, step):
                    units = pT[:, g % 2, first:UNITS_P, :].rearrange("p u n -> p (u n)")
                    view = units.rearrange("p (a n) -> p a n", n=step)[:, 0:count, col:col + P]
                    pool.affine_select(out=view, in_=view, compare_op=ALU.is_ge, fill=0.0, base=0,
                                       pattern=[[0, count], [1, P]], channel_multiplier=-1).then_inc(sel_done, 1)

                def low_qk(b, t):
                    s = t % 2
                    pool.wait_ge(hi_done, 6 * NT * b + PRIMED + 6 * (NT + t + 1))
                    pool.tensor_tensor(qtok[:, t, :, HD:2 * HD], rot[:, s, 0:HEADS, :], qtok[:, t, :, 0:HD].bitcast(F32),
                                       ALU.subtract).then_inc(lo_done, 1)
                    k_src = rot[:, s, HEADS:, :]
                    pool.tensor_tensor(ktok[:, t, :, 0, 2 * HD:3 * HD], k_src, ktok[:, t, :, 0, 0:HD].bitcast(F32), ALU.subtract)
                    pool.tensor_tensor(ktok[:, t, :, 1, 2 * HD:3 * HD], k_src, ktok[:, t, :, 1, 0:HD].bitcast(F32),
                                       ALU.subtract).then_inc(lo_done, 1)

                def move_values(b):
                    pool.wait_ge(v_done, NT * b + NT)
                    if live(b, -1):
                        pool.wait_ge(v_in, KV * b)
                    pool.sem_inc(pool_turn, 1)
                    staged = v_new if live(b, -1) else v_first
                    pool.tensor_copy(v_mid[:, :, :, :], staged[:, :, :, :]).then_inc(v_moved, 1)

                def take_values(b, g):
                    if g >= 0:
                        pool.wait_ge(v_moved, b + 1)
                    if live(b, g - 4):
                        pool.wait_ge(pv_done, PRIMED + KV * b + g - 3)
                    pool.sem_inc(pool_turn, 1)
                    pool.tensor_copy(vtok[:, :, g % KV, 0:HD], v_mid[:, :, g % KV, :]).then_inc(v_in, 1)

                def iteration(b):
                    for slot, i in STEPS:
                        if (slot, i) == (1, 0) and live(b, 0):
                            move_values(b)
                        if i == 0 and live(b, slot - 1):
                            take_values(b, slot - 1)
                        if live(b, slot - 2):
                            g = slot - 2
                            exps = KV * UNITS_P * b + UNITS_P * g
                            if i == 4:
                                wait_exp(exps + 4)
                                mask(g, 0, 4, 0, 512)
                            if i == 8:
                                wait_exp(exps + 8)
                                mask(g, 4, 4, 0, 512)
                                mask(g, 4, 4, 384, 512)
                            if i == 10:
                                wait_exp(exps + 10)
                                mask(g, 8, 4, 0, 256)
                        if (slot, i) in LOW_AT and present(("qkv",), b):
                            low_qk(b, LOW_AT.index((slot, i)))
                        if (slot, i) == DEVIATION_AT and present(("x",), b):
                            deviation(b + B + 1)

                iteration(-1)
                pipeline(pool, iteration)

            for s in primed["pool"]:
                pool.sem_inc(s, PRIMED)
            constants()
            pool.wait_ge(const, 6)
            deviation(0)
            padding()
            ffn(0, 0)
            attention()
            ffn(B, 2)


def rope_tables():
    import numpy as np
    inv = (np.float32(1.0) / np.float32(10000.0) ** (np.arange(0, HD, 2, dtype=np.float32) / np.float32(HD))).astype(np.float32)
    angle = (np.arange(T, dtype=np.float32)[:, None] * inv[None, :]).astype(np.float32)
    cos, sin = np.cos(angle), np.sin(angle)
    table = np.stack([np.concatenate([cos, cos], 1), np.concatenate([-sin, sin], 1)], 1)
    return np.ascontiguousarray(table.reshape(NT, P, 2, HD).transpose(1, 0, 2, 3)).astype(np.float32)


_INS = ["L0_attn_x", "L0_attn_Wq", "L0_attn_Wk", "L0_attn_Wv", "L0_attn_Wproj", "L0_ffn_wq_gate", "L0_ffn_s_gate",
        "L0_ffn_wq_up", "L0_ffn_s_up", "L0_ffn_wq_down", "L0_ffn_s_down"]


def kernel(**inputs):
    import numpy as np
    import concourse.bacc as bacc
    from concourse.bass_utils import run_bass_kernel_spmd as run

    nc = bacc.Bacc("TRN2", target_bir_lowering=False, num_devices=1)
    arrays = {f"{n}_dram": np.ascontiguousarray(inputs[n]) for n in _INS}
    arrays["rope_dram"] = rope_tables()
    args = [nc.dram_tensor(n, a.shape, mybir.dt.from_np(a.dtype), kind="ExternalInput").ap() for n, a in arrays.items()]
    out = nc.dram_tensor("out_dram", (B, T, C), F32, kind="ExternalOutput").ap()
    build(nc, *args, out)
    return run(nc, [arrays], core_ids=[0]).results[0]["out_dram"]
```
